# Optimizing a Trainium2 kernel written in Bass

```python
import numpy as np
import jax
import jax.numpy as jnp

def _softmax(x, axis=-1):
    return jax.nn.softmax(x, axis=axis)

def _gelu(x):
    return jax.nn.gelu(x, approximate=True)

def _silu(x):
    return jax.nn.silu(x)

def _sigmoid(x):
    return jax.nn.sigmoid(x)

def _layernorm(x, axis=-1, eps=1e-05):
    m = jnp.mean(x, axis=axis, keepdims=True)
    v = jnp.var(x, axis=axis, keepdims=True)
    return (x - m) / jnp.sqrt(v + eps)

def _scatter_add(tgt, idx, src, axis=0):
    return tgt.at[idx].add(src)

def _segment_sum(src, seg, n):
    return jax.ops.segment_sum(src, seg, n)
kernel_name = 'mk_adaln_ffn_d1_seqx_r4_321f85'

def setup_inputs(seed: int=0):
    np.random.seed(seed)
    _w = jnp.asarray

    def _rec_inputs():
        import jax
        import jax.numpy as jnp
        _rk = jax.random.key(seed)
        x = -0.000125 + 0.9999 * jax.random.normal(jax.random.fold_in(_rk, 1), (8, 256, 1024), jnp.float32)
        _lenS = 256 - jax.random.randint(jax.random.fold_in(_rk, 7), (8,), 0, max(1, 256 // 4) + 1, jnp.int32)
        _lenS2 = 256 - jax.random.randint(jax.random.fold_in(_rk, 8), (8,), 0, max(1, 256 // 4) + 1, jnp.int32)
        itok_B_3_7 = jax.random.randint(jax.random.fold_in(_rk, 11), (8,), 3, 8, jnp.int32)
        return (x, itok_B_3_7)
    x, itok_B_3_7 = _rec_inputs()

    def _L0_cond_setup():
        import jax, jax.numpy as jnp
        import numpy as np
        RANK = 16
        ALPHA = 16.0
        SCALING = ALPHA / RANK
        N_ADAPTERS = 8
        IN_F = 1024
        OUT_F = 1024
        BATCH = 4
        SEQ = 512
        key = jax.random.key(seed)
        kx, ka, kb, ki = jax.random.split(key, 4)
        x = jax.random.normal(kx, (BATCH, SEQ, IN_F), dtype=jnp.float32)
        A = jax.random.normal(ka, (N_ADAPTERS, OUT_F, RANK), dtype=jnp.float32) * 0.02
        B = jax.random.normal(kb, (N_ADAPTERS, RANK, IN_F), dtype=jnp.float32) * 0.02
        adapter_ids = jax.random.randint(ki, (BATCH,), 0, N_ADAPTERS, dtype=jnp.int32)
        return {'x': x, 'A': A, 'B': B, 'adapter_ids': adapter_ids}
    _L0_cond_all = _L0_cond_setup()
    _L0_cond_in = {k: v for k, v in _L0_cond_all.items() if k in ('A', 'B')}
    del _L0_cond_all

    def _L0_ffn_setup():
        import jax, jax.numpy as jnp
        import numpy as np
        TOP_K = 2
        key = jax.random.key(seed)
        k1, k2, k3 = jax.random.split(key, 3)
        B, S, H, O, E = (32, 1, 1024, 1024, 8)
        x = jax.random.normal(k1, (B, S, H), dtype=jnp.float32)
        gate_w = jax.random.normal(k2, (H, E), dtype=jnp.float32) * 0.02
        expert_w = jax.random.normal(k3, (E, H, O), dtype=jnp.float32) * 0.02
        return {'x': x, 'gate_w': gate_w, 'expert_w': expert_w}
    _L0_ffn_all = _L0_ffn_setup()
    _L0_ffn_in = {k: v for k, v in _L0_ffn_all.items() if k in ('gate_w', 'expert_w')}
    del _L0_ffn_all
    return {'x': x, 'itok_B_3_7': itok_B_3_7, 'L0_cond_A': _L0_cond_in['A'], 'L0_cond_B': _L0_cond_in['B'], 'L0_ffn_gate_w': _L0_ffn_in['gate_w'], 'L0_ffn_expert_w': _L0_ffn_in['expert_w']}

def reference(x, itok_B_3_7, L0_cond_A, L0_cond_B, L0_ffn_gate_w, L0_ffn_expert_w):
    import jax
    import jax.numpy as jnp

    def _L0_cond_ref(x, A, B, adapter_ids):
        import jax, jax.numpy as jnp
        import numpy as np
        RANK = 16
        ALPHA = 16.0
        SCALING = ALPHA / RANK
        N_ADAPTERS = 8
        IN_F = 1024
        OUT_F = 1024
        BATCH = 4
        SEQ = 512
        B_sel = B[adapter_ids]
        A_sel = A[adapter_ids]
        Bx = jnp.einsum('bni,bri->bnr', x, B_sel)
        out = jnp.einsum('bnr,bor->bno', Bx, A_sel)
        return out * SCALING

    def _L0_ffn_ref(x, gate_w, expert_w):
        import jax, jax.numpy as jnp
        import numpy as np
        TOP_K = 2
        E = expert_w.shape[0]
        gate_logits = jnp.einsum('bsh,he->bse', x, gate_w)
        top_vals, top_idx = jax.lax.top_k(gate_logits, TOP_K)
        probs = jax.nn.softmax(top_vals, axis=-1)
        onehot = jax.nn.one_hot(top_idx, E, dtype=x.dtype)
        w_e = jnp.einsum('bsk,bske->bse', probs, onehot)
        expert_out = jnp.einsum('bsh,eho->bseo', x, expert_w)
        out = jnp.einsum('bseo,bse->bso', expert_out, w_e)
        return out
    x = x + _L0_ffn_ref(_L0_cond_ref(x, L0_cond_A, L0_cond_B, itok_B_3_7), L0_ffn_gate_w, L0_ffn_expert_w)
    return x

_drawn_inputs = setup_inputs


def setup_inputs(seed=0):
    import zlib

    import numpy as np

    out = dict(_drawn_inputs(seed))
    spreads = {}
    factors = {}
    for name, (base, spread) in spreads.items():
        noise = np.random.default_rng([zlib.crc32(name.encode()), seed]).standard_normal(out[name].shape)
        drawn = base * np.exp(spread * noise) if base else spread * noise
        out[name] = jnp.asarray(drawn.astype(out[name].dtype))
    for name, factor in factors.items():
        out[name] = (out[name] * factor).astype(out[name].dtype)
    return out
```

```python
from contextlib import ExitStack

import concourse.bass as bass
from concourse import mybir


P = 128
Q = 32
F32 = mybir.dt.float32
F32R = mybir.dt.float32r
I32 = mybir.dt.int32
U32 = mybir.dt.uint32
ALU = mybir.AluOpType
ACT = mybir.ActivationFunctionType
AX_X = mybir.AxisListType.X
TOP = 2
LANES8 = 8
DMA = 16
ROUTE_OPS = 15
GAP_OP = 5
PICK_STEPS = 5
LAG = 2
WARM_UP = 16


def adaln_ffn(nc, x, ids, A, B, gate_w, W, out):
    NB, S, D = x.shape
    NA, H, R = A.shape
    E, _, O = W.shape
    J = S // P
    C = D // P
    CG = C // 2
    K = H // P
    HALF = K // 2
    N = 512
    BLOCKS = O // N
    PAIRS = E // 2
    STEPS = BLOCKS * E
    RG = R + E
    BANKS = 4
    assert NA * R == P and E * R == P and 2 * R == Q and NB == E and E == LANES8 and J == 2 and BLOCKS == 2

    x_dram = x.rearrange("b (p j) i -> p b j i", j=J)
    out_dram = out.rearrange("b (p j) o -> p b j o", j=J)
    A_dram = A.rearrange("a (p k) r -> p a (k r)", k=K)
    W_dram = W.rearrange("e (p k) o -> p e k o", k=K)
    gate_dram = gate_w.rearrange("(p k) e -> p (k e)", k=K)

    with ExitStack() as ctx:
        def sb(name, shape, dt=F32):
            return ctx.enter_context(nc.sbuf_tensor(name, shape, dt))

        def bank(name, shape):
            return ctx.enter_context(nc.psum_tensor(name, shape, F32))

        def sem(name):
            return ctx.enter_context(nc.semaphore(name))

        ids_sb = sb("ids_sb", [P, NB], I32)
        ids_f = sb("ids_f", [P, NB])
        odd_i = sb("odd_i", [P, NB], I32)
        odd_f = sb("odd_f", [P, NB])
        ident = sb("ident", [P, P])
        row_no = sb("row_no", [P, 1])
        count_up = sb("count_up", [P, R])
        other = sb("other", [P, E])
        row_of = sb("row_of", [P, NB])
        pick = sb("pick", [P, NB * R + NB * E])
        picked = sb("picked", [P, NB])
        slot_expert = sb("slot_expert", [P, NB, E])
        A_sb = sb("A_sb", [P, NA, K * R])
        A_T = [sb(f"A_T{v}", [P, K, P]) for v in range(2)]
        B_sb = sb("B_sb", [P, D])
        gate_sb = sb("gate_sb", [P, K * E])
        BG = sb("BG", [P, NB, C, 2 * RG], F32R)
        BG_now = [sb(f"BG_now{q}", [P, C, 2 * RG], F32R) for q in range(2)]
        fold = sb("fold", [2 * RG, RG])
        W_sb = [sb(f"W_sb{n}", [P, HALF, N]) for n in range(4)]
        M_sb = sb("M_sb", [P, BLOCKS * NA, N])
        x_in = [sb(f"x_in{q}", [P, J, D]) for q in range(2)]
        x_keep = sb("x_keep", [P, NB, J, D])
        xT_high = sb("xT_high", [P, C, J * P], F32R)
        xT_low = sb("xT_low", [P, C, J * P], F32R)
        BxT = sb("BxT", [2 * RG, J * P])
        Bx = [sb(f"Bx{q}", [P, J, RG]) for q in range(2)]
        top = sb("top", [P, J, LANES8])
        top_no = sb("top_no", [P, J, LANES8], U32)
        top_nof = sb("top_nof", [P, J, TOP])
        gap = sb("gap", [P, J])
        exp_gap = sb("exp_gap", [P, J])
        total = sb("total", [P, J])
        prob = sb("prob", [P, J, TOP])
        hot = sb("hot", [P, J, TOP, E])
        w_e = sb("w_e", [P, J, E])
        G = [sb(f"G{q}", [P, J, E, R]) for q in range(2)]
        GT = sb("GT", [P, NB, J * P])
        GT_now = [sb(f"GT_now{q}", [P, J, P]) for q in range(2)]

        ps_P = bank("ps_P", [P, BANKS, N])
        ps_X = [bank(f"ps_X{g}", [P, N]) for g in range(2)]
        ps_B = [bank(f"ps_B{q}", [P, N]) for q in range(2)]
        BX_AT = J * P
        ps_F = [ps_X, ps_B]
        BG_banks = (ps_P[:, 2, :], ps_P[:, 3, :], ps_B[1], ps_B[0])

        A_landed = sem("A_landed")
        B_landed = sem("B_landed")
        ids_landed = sem("ids_landed")
        gate_landed = sem("gate_landed")
        x_landed = [sem(f"x_landed{q}") for q in range(2)]
        W_landed = [sem(f"W_landed{n}") for n in range(4)]
        zeroed = sem("zeroed")
        fold_made = sem("fold_made")
        consts_made = sem("consts_made")
        A_turned = sem("A_turned")
        picks = sem("picks")
        AG_done = sem("AG_done")
        BG_done = sem("BG_done")
        BG_high = sem("BG_high")
        BG_low = sem("BG_low")
        xT_done = sem("xT_done")
        xT_highs = sem("xT_highs")
        xT_lows = sem("xT_lows")
        BG_staged = sem("BG_staged")
        BxT_done = sem("BxT_done")
        BxT_copied = sem("BxT_copied")
        x_kept = sem("x_kept")
        Bx_done = sem("Bx_done")
        routed = sem("routed")
        exp_done = sem("exp_done")
        GT_done = sem("GT_done")
        GT_copied = sem("GT_copied")
        GT_staged = sem("GT_staged")
        W_used = sem("W_used")
        slots_freed = sem("slots_freed")
        odd_rows = sem("odd_rows")
        even_rows = sem("even_rows")
        last_wholes = sem("last_wholes")
        F_done = sem("F_done")
        F_added = sem("F_added")
        stored = [sem(f"stored{blk}") for blk in range(2)]

        block = ctx.enter_context(nc.Block())

        def whole(copy, pair, j, odd_adapter):
            blk, i = pair // PAIRS, pair % PAIRS
            n = (2 * pair + (0 if odd_adapter else 1)) % BANKS
            return copy(M_sb[Q * i:Q * i + Q, blk * NA + 2 * j + odd_adapter, :], ps_P[Q * j:Q * j + Q, n, :])

        def first_half(copy, pair, j, odd_adapter):
            blk, i = pair // PAIRS, pair % PAIRS
            n = (2 * pair + (1 if odd_adapter else 0)) % BANKS
            return copy(M_sb[Q * i:Q * i + R, blk * NA + 2 * j + odd_adapter, :], ps_P[Q * j:Q * j + R, n, :])

        def store(engine, b, blk):
            columns = slice(blk * N, (blk + 1) * N)
            engine.dma_start(out_dram[:, bass.ds(b, 1), :, columns].rearrange("p b j n -> p (b j) n"),
                             x_keep[:, bass.ds(b, 1), :, columns].rearrange("p b j n -> p (b j) n")
                             ).then_inc(stored[blk], DMA)

        @block.sync
        def _(sp):
            def place(trip, q):
                step = trip * 2 + q
                return step & (E - 1), ((step >> (E.bit_length() - 1)) & (BLOCKS - 1)) * N

            def load_W(e, column, q, half):
                n = 2 * q + half
                sp.dma_start(W_sb[n][:],
                             W_dram[:, bass.ds(e, 1), half * HALF:(half + 1) * HALF, bass.ds(column, N)]
                             .rearrange("p e k o -> p (e k) o")).then_inc(W_landed[n], DMA)

            def load_x(b, q):
                sp.dma_start(x_in[q][:], x_dram[:, bass.ds(b, 1)].rearrange("p b j i -> p (b j) i")
                             ).then_inc(x_landed[q], DMA)

            def load_ahead(trip, with_x):
                for q in range(2):
                    e, column = (sp.snap(v) for v in place(trip, q))
                    for half in range(2):
                        sp.wait_ge(W_used, trip * 4 + (2 * q + half - 3))
                        sp.sem_inc(slots_freed, 1)
                        load_W(e, column, q, half)
                    if with_x:
                        b = trip * 2 + q
                        sp.wait_ge(x_kept, b - 1)
                        sp.sem_inc(slots_freed, 1)
                        sp.wait_ge(xT_done, b * (2 * J) - 2 * J)
                        sp.sem_inc(slots_freed, 1)
                        load_x(b, q)

            sp.dma_start(A_sb[:], A_dram).then_inc(A_landed, DMA)
            load_W(0, 0, 0, 0)
            sp.dma_start(gate_sb[:], gate_dram).then_inc(gate_landed, DMA)
            sp.dma_start(B_sb[:], B.rearrange("a r i -> (a r) i")).then_inc(B_landed, DMA)
            load_W(0, 0, 0, 1)
            load_x(0, 0)
            load_W(1, 0, 1, 0)
            load_W(1, 0, 1, 1)
            load_x(1, 1)
            with sp.Fori(1, PAIRS) as trip:
                load_ahead(trip, True)
            with sp.Fori(PAIRS, STEPS // 2) as trip:
                load_ahead(trip, False)

            for blk, first in ((0, NB - LAG - 2), (1, NB)):
                with sp.Fori(first, NB * (blk + 1)) as u:
                    sp.wait_ge(F_added, u * J + J)
                    sp.sem_inc(slots_freed, 1)
                    store(sp, u - blk * NB, blk)
            sp.wait_ge(stored[0], NB * DMA)
            sp.wait_ge(stored[1], NB * DMA)

        @block.gpsimd
        def _(pool):
            nc.gpsimd.memset(ident[:], 0.0).then_inc(zeroed, 1)
            nc.gpsimd.memset(fold[:], 0.0).then_inc(zeroed, 1)
            pool.wait_ge(zeroed, 2)
            nc.gpsimd.affine_select(out=ident[:], in_=ident[:], compare_op=ALU.not_equal, fill=1.0, base=0,
                                    pattern=[[-1, P]], channel_multiplier=1).then_inc(consts_made, 1)
            nc.gpsimd.iota(row_no[:], pattern=[[0, 1]], base=0, channel_multiplier=1,
                           allow_small_or_imprecise_dtypes=True).then_inc(consts_made, 1)
            nc.gpsimd.iota(count_up[:], pattern=[[1, R]], base=0, channel_multiplier=0,
                           allow_small_or_imprecise_dtypes=True).then_inc(consts_made, 1)
            for half, value in enumerate((1.0, -1.0)):
                nc.gpsimd.memset(other[:].rearrange("p (i h) -> p i h", h=2)[:, :, half], value).then_inc(consts_made, 1)

            for n in range(2):
                nc.gpsimd.affine_select(out=fold[:], in_=fold[:], compare_op=ALU.not_equal, fill=1.0, base=-n * RG,
                                        pattern=[[-1, RG]], channel_multiplier=1).then_inc(fold_made, 1)
                pool.wait_ge(fold_made, n + 1)

            def stage_BG(b, q):
                nc.gpsimd.tensor_copy(BG_now[q][:].rearrange("p c n -> p (c n)"),
                                      BG[:, bass.ds(b, 1), :, :].rearrange("p b c n -> p (b c n)")).then_inc(BG_staged, 1)

            def keep_x(trip, q):
                pool.wait_ge(x_landed[q], trip * DMA + DMA)
                nc.gpsimd.tensor_copy(x_keep[:, bass.ds(trip * 2 + q, 1), :, :].rearrange("p b j i -> p (b j) i"),
                                      x_in[q][:]).then_inc(x_kept, 1)

            pool.wait_ge(BG_low, 2 * len(BG_banks))
            for q in range(2):
                stage_BG(q, q)
                keep_x(0, q)
            with pool.Fori(1, NB // 2) as trip:
                for q in range(2):
                    pool.wait_ge(BxT_done, trip * 2 + (q - 1))
                    stage_BG(trip * 2 + q, q)
                    keep_x(trip, q)

        @block.scalar
        def _(act):
            act.dma_start(ids_sb[:], ids.rearrange("(a b) -> a b", a=1).to_broadcast([P, NB])).then_inc(ids_landed, DMA)

            def high_BG():
                for n, ps in enumerate(BG_banks):
                    act.wait_ge(BG_done, n + 1)
                    v = ps[:, 0:2 * (P + NB * E)].rearrange("p (c n) -> p c n", c=2)
                    nc.scalar.copy(BG[:, :, 2 * n:2 * n + 2, 0:R],
                                   v[:, :, 0:P].rearrange("p c (b r) -> p b c r", b=NB)).then_inc(BG_high, 1)
                    nc.scalar.copy(BG[:, :, 2 * n:2 * n + 2, R:RG],
                                   v[:, :, P:].rearrange("p c (b e) -> p b c e", b=NB)).then_inc(BG_high, 1)

            def high_xT(b, j):
                for g in range(2):
                    act.wait_ge(xT_done, (b * J + j) * 2 + g + 1)
                    nc.scalar.copy(xT_high[:, g * CG:(g + 1) * CG, j * P:(j + 1) * P],
                                   ps_X[g][:].rearrange("p (c t) -> p c t", c=CG)).then_inc(xT_highs, 1)

            def odd_adapters(pair, part):
                if part is whole:
                    act.wait_ge(W_used, 4 * pair + 4)
                else:
                    act.wait_ge(odd_rows, 2 * pair + 1)
                    act.wait_ge(even_rows, 2 * pair + 1)
                for j in range(PAIRS):
                    last = part(nc.scalar.copy, pair, j, 1)
                last.then_inc(odd_rows, 1)

            def odd_adapters_after(step):
                if step >= 1:
                    odd_adapters((step - 1) // 2, whole if step % 2 else first_half)

            def copy_GT(b):
                act.wait_ge(GT_done, b + 1)
                nc.scalar.copy(GT[:, b, :], ps_B[b % 2][:, 0:J * P]).then_inc(GT_copied, 1)

            def exps(b):
                act.wait_ge(routed, b * ROUTE_OPS + GAP_OP)
                nc.scalar.activation(exp_gap[:], gap[:], ACT.Exp).then_inc(exp_done, 1)

            def copy_BxT(b):
                act.wait_ge(BxT_done, b + 1)
                nc.scalar.copy(BxT[:], ps_B[b % 2][0:2 * RG, 0:J * P]).then_inc(BxT_copied, 1)

            def stage_GT(u):
                if u >= 2:
                    act.wait_ge(F_done, (u - 1) * J)
                nc.scalar.copy(GT_now[u % 2][:].rearrange("p j t -> p (j t)"), GT[:, u % NB, :]).then_inc(GT_staged, 1)

            high_BG()
            for b in range(NB):
                if b:
                    copy_BxT(b - 1)
                high_xT(b, 0)
                if b:
                    exps(b - 1)
                odd_adapters_after(b)
                high_xT(b, 1)
                if b:
                    copy_GT(b - 1)
            copy_BxT(NB - 1)
            exps(NB - 1)
            odd_adapters_after(E)
            copy_GT(NB - 1)
            act.wait_ge(GT_copied, NB)
            for step in range(E + 1, STEPS - 1):
                odd_adapters_after(step)
                u = step - E - LAG
                if u + 1 >= 0:
                    stage_GT(u + 1)
                if u - 1 >= 0:
                    act.wait_ge(F_added, u * J)
                    store(act, u - 1, 0)
            pair = STEPS // 2 - 1
            act.wait_ge(W_used, 4 * pair + 2)
            for j in range(PAIRS):
                last = whole(nc.scalar.copy, pair, j, 1)
            last.then_inc(odd_rows, 1)
            act.wait_ge(odd_rows, 2 * pair + 1)
            stage_GT(NB - LAG)
            for j in range(PAIRS):
                act.wait_ge(last_wholes, j + 1)
                last = first_half(nc.scalar.copy, pair, j, 1)
            stage_GT(NB - LAG + 1)
            for j in range(PAIRS // 2, PAIRS):
                last = first_half(nc.scalar.copy, pair, j, 0)
            last.then_inc(odd_rows, 1)
            for u in range(NB, 2 * NB):
                stage_GT(u)

        @block.vector
        def _(dve):
            done = [0]

            def pick_step(ins):
                done[0] += 1
                ins.then_inc(picks, 1)
                dve.wait_ge(picks, done[0])

            dve.wait_ge(A_landed, DMA)
            turned = A_sb[:].rearrange("p (j h) (k r) -> p k j h r", h=2, k=K)
            nc.vector.tensor_copy(A_T[0][:].rearrange("p k (a r) -> p k a r", a=NA),
                                  A_sb[:].rearrange("p a (k r) -> p k a r", k=K)).then_inc(A_turned, 1)
            for h in range(2):
                nc.vector.tensor_copy(A_T[1][:].rearrange("p k (j h r) -> p k j h r", h=2, r=R)[:, :, :, h, :],
                                      turned[:, :, :, 1 - h, :]).then_inc(A_turned, 1)

            dve.wait_ge(consts_made, 5)
            dve.wait_ge(ids_landed, DMA)
            pick_step(nc.vector.tensor_copy(ids_f[:], ids_sb[:]))
            pick_step(nc.vector.tensor_scalar(row_of[:], ids_f[:], float(-R), row_no[:, 0:1], ALU.mult, ALU.add))
            pick_r = pick[:, 0:NB * R].rearrange("p (b r) -> p b r", b=NB)
            pick_step(nc.vector.tensor_tensor(pick_r, row_of[:].unsqueeze(2).to_broadcast([P, NB, R]),
                                              count_up[:].unsqueeze(1).to_broadcast([P, NB, R]), ALU.is_equal))
            pick_step(nc.vector.tensor_reduce(picked[:], pick_r, AX_X, ALU.add))
            dve.wait_ge(AG_done, 1)
            pick_step(nc.vector.tensor_tensor(pick[:, NB * R:].rearrange("p (b e) -> p b e", b=NB),
                                              ps_B[0][:, 0:E].unsqueeze(1).to_broadcast([P, NB, E]),
                                              picked[:].unsqueeze(2).to_broadcast([P, NB, E]), ALU.mult))
            assert done[0] == PICK_STEPS
            pick_step(nc.vector.tensor_scalar(odd_i[:], ids_sb[:], 1, None, ALU.bitwise_and))
            pick_step(nc.vector.tensor_copy(odd_f[:], odd_i[:]))
            pick_step(nc.vector.tensor_tensor(slot_expert[:], odd_f[:].unsqueeze(2).to_broadcast([P, NB, E]),
                                              other[:].unsqueeze(1).to_broadcast([P, NB, E]), ALU.mult))
            pick_step(nc.vector.tensor_tensor(slot_expert[:], slot_expert[:],
                                              count_up[:, 0:E].unsqueeze(1).to_broadcast([P, NB, E]), ALU.add))

            def low_BG():
                for n, ps in enumerate(BG_banks):
                    v = ps[:, 0:2 * (P + NB * E)].rearrange("p (c n) -> p c n", c=2)
                    for lo, hi, src in ((0, R, v[:, :, 0:P]), (R, RG, v[:, :, P:])):
                        dve.wait_ge(BG_high, 2 * n + 2)
                        nc.vector.tensor_tensor(BG[:, :, 2 * n:2 * n + 2, RG + lo:RG + hi],
                                                src.rearrange("p c (b n) -> p b c n", b=NB),
                                                BG[:, :, 2 * n:2 * n + 2, lo:hi],
                                                ALU.subtract).then_inc(BG_low, 1)

            def low_xT(b, j):
                for g in range(2):
                    dve.wait_ge(xT_highs, (b * J + j) * 2 + g + 1)
                    at = (slice(None), slice(g * CG, (g + 1) * CG), slice(j * P, (j + 1) * P))
                    nc.vector.tensor_tensor(xT_low[at], ps_X[g][:].rearrange("p (c t) -> p c t", c=CG),
                                            xT_high[at], ALU.subtract).then_inc(xT_lows, 1)

            def route(b):
                q = b % 2
                n = [0]

                def step(ins):
                    n[0] += 1
                    ins.then_inc(routed, 1)

                def steps_done():
                    dve.wait_ge(routed, b * ROUTE_OPS + n[0])

                dve.wait_ge(Bx_done, b + 1)
                step(nc.vector.tensor_copy(Bx[q][:],
                                           ps_B[q][:, BX_AT:BX_AT + J * RG].rearrange("p (j n) -> p j n", j=J)))
                steps_done()
                step(nc.vector.memset(total[:], 1.0))
                for j in range(J):
                    step(nc.vector.max(top[:, j, :], Bx[q][:, j, R:RG]))
                steps_done()
                step(nc.vector.tensor_tensor(gap[:], top[:, :, 1], top[:, :, 0], ALU.subtract))
                for j in range(J):
                    step(nc.vector.max_index(top_no[:, j, :], top[:, j, :], Bx[q][:, j, R:RG]))
                steps_done()
                step(nc.vector.tensor_copy(top_nof[:], top_no[:, :, 0:TOP]))
                steps_done()
                hot_jk = hot[:].rearrange("p j k e -> p (j k) e")
                step(nc.vector.tensor_tensor(hot_jk,
                                             slot_expert[:, b, :].unsqueeze(1).to_broadcast([P, J * TOP, E]),
                                             top_nof[:].rearrange("p j k -> p (j k)").unsqueeze(2)
                                             .to_broadcast([P, J * TOP, E]), ALU.is_equal))
                dve.wait_ge(exp_done, b + 1)
                step(nc.vector.tensor_tensor(total[:], total[:], exp_gap[:], ALU.add))
                steps_done()
                step(nc.vector.reciprocal(prob[:, :, 0], total[:]))
                steps_done()
                step(nc.vector.tensor_tensor(prob[:, :, 1], prob[:, :, 0], exp_gap[:], ALU.mult))
                steps_done()
                step(nc.vector.tensor_tensor(hot_jk, hot_jk, prob[:].rearrange("p j k -> p (j k)").unsqueeze(2)
                                             .to_broadcast([P, J * TOP, E]), ALU.mult))
                steps_done()
                step(nc.vector.tensor_tensor(w_e[:], hot[:, :, 0, :], hot[:, :, 1, :], ALU.add))
                steps_done()
                for j in range(J):
                    last = nc.vector.tensor_tensor(G[q][:, j, :, :],
                                                   Bx[q][:, j, 0:R].unsqueeze(1).to_broadcast([P, E, R]),
                                                   w_e[:, j, :].unsqueeze(2).to_broadcast([P, E, R]), ALU.mult)
                step(last)
                assert n[0] == ROUTE_OPS

            def even_adapters(pair, part):
                if part is whole:
                    dve.wait_ge(W_used, 4 * pair + 4)
                else:
                    dve.wait_ge(even_rows, 2 * pair + 1)
                    dve.wait_ge(odd_rows, 2 * pair + 1)
                for j in range(PAIRS):
                    last = part(nc.vector.tensor_copy, pair, j, 0)
                last.then_inc(even_rows, 1)

            def even_adapters_after(step):
                if step >= 1:
                    even_adapters((step - 1) // 2, whole if step % 2 else first_half)

            def add(u, q, blk):
                b = u - blk * NB
                for j in range(J):
                    dve.wait_ge(F_done, u * J + (j + 1))
                    v = x_keep[:, bass.ds(b, 1), j, blk * N:(blk + 1) * N].rearrange("p b n -> p (b n)")
                    nc.vector.tensor_tensor(v, v, ps_F[q][j][:], ALU.add).then_inc(F_added, 1)

            low_BG()
            for b in range(NB):
                low_xT(b, 0)
                if b:
                    route(b - 1)
                even_adapters_after(b)
                low_xT(b, 1)
            route(NB - 1)
            even_adapters_after(E)
            dve.wait_ge(x_kept, NB)
            for step in range(E + 1, STEPS - 1):
                even_adapters_after(step)
                if step - E >= LAG:
                    add(step - E - LAG, step % 2, 0)
            last_pair = STEPS // 2 - 1
            dve.wait_ge(W_used, 2 * STEPS)
            for j in range(PAIRS):
                whole(nc.vector.tensor_copy, last_pair, j, 0).then_inc(last_wholes, 1)
            dve.wait_ge(last_wholes, PAIRS)
            add(NB - LAG - 1, (NB - LAG - 1) % 2, 0)
            dve.wait_ge(odd_rows, 2 * last_pair + 1)
            for j in range(PAIRS // 2):
                last = first_half(nc.vector.tensor_copy, last_pair, j, 0)
            last.then_inc(even_rows, 1)
            for u in range(NB - LAG, NB):
                add(u, u % 2, 0)
            with dve.Fori(PAIRS, 2 * PAIRS) as trip:
                for q in range(2):
                    add(trip * 2 + q, q, 1)

        @block.tensor
        def _(pe):
            def experts_product(trip, q, half, waits):
                step = trip * 2 + q
                n = 2 * q + half
                out_bank = ps_P[:, bass.ds((trip & 1) * 2 + q, 1), :].rearrange("p b n -> p (b n)")
                if waits and (q, half) == (0, 0):
                    pe.wait_ge(odd_rows, trip * 2 - 2)
                    pe.wait_ge(even_rows, trip * 2 - 2)
                pe.wait_ge(W_landed[n], trip * DMA + DMA)
                for k in range(HALF):
                    kk = half * HALF + k
                    last = nc.tensor.matmul(out_bank, A_T[q][:, kk, :], W_sb[n][:, k, :],
                                            start=(kk == 0), stop=(kk == K - 1))
                last.then_inc(W_used, 1)

            def x_transposes(trip, q, j):
                b = trip * 2 + q
                if j == 0:
                    pe.wait_ge(x_landed[q], trip * DMA + DMA)
                for g in range(2):
                    if not (isinstance(b, int) and b == 0 and j == 0):
                        pe.wait_ge(xT_lows, b * (2 * J) + (2 * j + g - 1))
                    for c in range(CG):
                        cc = g * CG + c
                        last = nc.tensor.transpose(ps_X[g][:, c * P:(c + 1) * P],
                                                   x_in[q][:, j, cc * P:(cc + 1) * P], ident[:])
                    last.then_inc(xT_done, 1)

            def BxT_product(trip, q):
                b = trip * 2 + q
                pe.wait_ge(BG_staged, b + 1)
                pe.wait_ge(xT_lows, b * (2 * J) + 2 * J)
                if not (isinstance(trip, int) and trip == 0):
                    pe.wait_ge(GT_copied, b - 1)
                for c in range(C):
                    for part in (xT_high, xT_low):
                        last = nc.tensor.matmul(ps_B[q][0:2 * RG, 0:J * P], BG_now[q][:, c, :], part[:, c, :],
                                                start=(c == 0 and part is xT_high),
                                                stop=(c == C - 1 and part is xT_low))
                last.then_inc(BxT_done, 1)

            def Bx_product(b, q):
                pe.wait_ge(BxT_copied, b + 1)
                for j in range(J):
                    last = nc.tensor.matmul(ps_B[q][:, BX_AT + j * RG:BX_AT + (j + 1) * RG],
                                            BxT[:, j * P:(j + 1) * P], fold[:], start=True, stop=True)
                last.then_inc(Bx_done, 1)

            def g_transposes(b, q):
                pe.wait_ge(routed, b * ROUTE_OPS + ROUTE_OPS)
                for j in range(J):
                    last = nc.tensor.transpose(ps_B[q][:, j * P:(j + 1) * P],
                                               G[q][:, j, :, :].rearrange("p e r -> p (e r)"), ident[:])
                last.then_inc(GT_done, 1)

            def x_step(trip, q, first):
                experts = (trip, 1) if q == 0 else (trip + 1, 0)
                x_transposes(trip, q, 0)
                if not first:
                    Bx_product(trip * 2 + (q - 1), 1 - q)
                experts_product(*experts, 0, not (isinstance(trip, int) and trip == 0))
                x_transposes(trip, q, 1)
                experts_product(*experts, 1, False)
                if not first:
                    g_transposes(trip * 2 + (q - 1), 1 - q)
                BxT_product(trip, q)

            def final(trip, q, blk, waits):
                u = trip * 2 + q
                a = pe.value_load(ids_sb[0:1, bass.ds(u - blk * NB, 1)], min_val=0, max_val=NA - 1)
                pe.wait_ge(GT_staged, u + 1)
                for j in range(J):
                    if waits:
                        pe.wait_ge(F_added, u * J + (j + 1 - 2 * J))
                    nc.tensor.matmul(ps_F[q][j][:], GT_now[q][:, j, :],
                                     M_sb[:, bass.ds(a + blk * NA, 1), :].rearrange("p b n -> p (b n)"),
                                     start=True, stop=True).then_inc(F_done, 1)

            pe.wait_ge(consts_made, 5)
            for _ in range(WARM_UP):
                nc.tensor.matmul(ps_X[0][:, 0:P], ident[:], ident[:], start=True, stop=True)

            pe.wait_ge(A_turned, 1)
            experts_product(0, 0, 0, False)
            pe.wait_ge(gate_landed, DMA)
            for k in range(K):
                last = nc.tensor.matmul(ps_B[0][:, 0:E], A_T[0][:, k, :], gate_sb[:, k * E:(k + 1) * E],
                                        start=(k == 0), stop=(k == K - 1))
            last.then_inc(AG_done, 1)
            experts_product(0, 0, 1, False)
            pe.wait_ge(B_landed, DMA)
            pe.wait_ge(picks, PICK_STEPS)
            for n, ps in enumerate(BG_banks):
                for c in range(2):
                    at = c * (P + NB * E)
                    last = nc.tensor.matmul(ps[:, at:at + P + NB * E], B_sb[:, (2 * n + c) * P:(2 * n + c + 1) * P],
                                            pick[:], start=True, stop=True)
                last.then_inc(BG_done, 1)

            pe.wait_ge(A_turned, 3)
            pe.wait_ge(fold_made, 2)
            for q in range(2):
                x_step(0, q, q == 0)
            with pe.Fori(1, PAIRS) as trip:
                for q in range(2):
                    x_step(trip, q, False)

            Bx_product(NB - 1, 1)
            for half in range(2):
                experts_product(PAIRS, 1, half, True)
            g_transposes(NB - 1, 1)

            def block1_trip(trip, final_waits):
                for q in range(2):
                    for half in range(2):
                        experts_product(trip, q, half, True)
                    final(trip - (PAIRS + LAG // 2), q, 0, final_waits)

            pe.wait_ge(ids_landed, DMA)
            block1_trip(PAIRS + 1, False)
            with pe.Fori(PAIRS + 2, 2 * PAIRS) as trip:
                block1_trip(trip, True)
            for q in range(2):
                final(PAIRS - 1, q, 0, True)
            pe.wait_ge(odd_rows, STEPS)
            pe.wait_ge(even_rows, STEPS - 1)
            with pe.Fori(PAIRS, 2 * PAIRS) as trip:
                for q in range(2):
                    final(trip, q, 1, True)


def kernel(x, itok_B_3_7, L0_cond_A, L0_cond_B, L0_ffn_gate_w, L0_ffn_expert_w):
    import numpy as np
    import concourse.bacc as bacc
    from concourse.bass_utils import run_bass_kernel_spmd

    nc = bacc.Bacc("TRN2", target_bir_lowering=False, num_devices=1)
    given = {"x": x, "ids": itok_B_3_7, "A": L0_cond_A, "B": L0_cond_B, "gate_w": L0_ffn_gate_w,
             "W": L0_ffn_expert_w}
    arrays, args = {}, []
    for name, a in given.items():
        a = np.ascontiguousarray(a)
        arrays[f"{name}_dram"] = a
        args.append(nc.dram_tensor(f"{name}_dram", a.shape, mybir.dt.from_np(a.dtype), kind="ExternalInput").ap())
    result = nc.dram_tensor("out_dram", arrays["x_dram"].shape, F32, kind="ExternalOutput").ap()
    adaln_ffn(nc, *args, result)
    r = run_bass_kernel_spmd(nc, [arrays], core_ids=[0])
    return r.results[0]["out_dram"]
```

```python
from contextlib import ExitStack

import concourse.bass as bass
from concourse import mybir


P = 128
Q = 32
F32 = mybir.dt.float32
I32 = mybir.dt.int32
U32 = mybir.dt.uint32
ALU = mybir.AluOpType
ACT = mybir.ActivationFunctionType
AX_X = mybir.AxisListType.X
TOP = 2
LANES8 = 8
DMA = 16
ROUTE_OPS = 15
GAP_OP = 5
PICK_STEPS = 6
LAG = 2
BEGIN = 2
WARM_UP = 7
KEEP_WARM = 2


def adaln_ffn(nc, x, ids, A, B, gate_w, W, out):
    NB, S, D = x.shape
    NA, H, R = A.shape
    E, _, O = W.shape
    J = S // P
    C = D // P
    CG = C // 2
    K = H // P
    HALF = K // 2
    N = 512
    BLOCKS = O // N
    PAIRS = E // 2
    STEPS = BLOCKS * E
    RG = R + E
    BANKS = 4
    QUADS = P // Q
    assert RG <= Q and C % QUADS == 0
    assert NA * R == P and E * R == P and 2 * R == Q and NB == E and E == LANES8 and J == 2 and BLOCKS == 2

    x_dram = x.rearrange("b (p j) i -> p b j i", j=J)
    out_dram = out.rearrange("b (p j) o -> p b j o", j=J)
    A_dram = A.rearrange("a (p k) r -> p a (k r)", k=K)
    W_dram = W.rearrange("e (p k) o -> p e k o", k=K)
    gate_dram = gate_w.rearrange("(p k) e -> p k e", k=K)

    with ExitStack() as ctx:
        def sb(name, shape, dt=F32):
            return ctx.enter_context(nc.sbuf_tensor(name, shape, dt))

        def bank(name, shape):
            return ctx.enter_context(nc.psum_tensor(name, shape, F32))

        def sem(name):
            return ctx.enter_context(nc.semaphore(name))

        ids_sb = sb("ids_sb", [P, NB], I32)
        ids_f = sb("ids_f", [P, NB])
        odd_i = sb("odd_i", [P, NB], I32)
        odd_f = sb("odd_f", [P, NB])
        ident = sb("ident", [P, P])
        row_no = sb("row_no", [P, 1])
        count_up = sb("count_up", [P, R])
        other = sb("other", [P, E])
        row_of = sb("row_of", [P, NB])
        pick = sb("pick", [P, NB * R + NB * E])
        picked = sb("picked", [P, NB])
        slot_expert = sb("slot_expert", [P, NB, E])
        A_sb = sb("A_sb", [P, NA, K * R])
        A_T = [sb(f"A_T{v}", [P, K, P]) for v in range(2)]
        B_sb = sb("B_sb", [P, D])
        gate_sb = sb("gate_sb", [P, K, E])
        gate_wide = sb("gate_wide", [P, K, Q])
        AG = sb("AG", [P, E])
        AG_T = sb("AG_T", [P, P])
        BG = sb("BG", [P, NB, C, Q])
        BG_now = [sb(f"BG_now{q}", [P, C, Q]) for q in range(2)]
        W_sb = [sb(f"W_sb{n}", [P, HALF, N]) for n in range(4)]
        M_sb = sb("M_sb", [P, BLOCKS * NA, N])
        x_in = [sb(f"x_in{q}", [P, J, D]) for q in range(2)]
        x_keep = sb("x_keep", [P, NB, J, D])
        xT = sb("xT", [P, C, J * P])
        BxT = sb("BxT", [P, J * P])
        Bx = [sb(f"Bx{q}", [P, J, RG]) for q in range(2)]
        top = sb("top", [P, J, LANES8])
        top_no = sb("top_no", [P, J, LANES8], U32)
        top_nof = sb("top_nof", [P, J, TOP])
        gap = sb("gap", [P, J])
        exp_gap = sb("exp_gap", [P, J])
        total = sb("total", [P, J])
        prob = sb("prob", [P, J, TOP])
        hot = sb("hot", [P, J, TOP, E])
        w_e = sb("w_e", [P, J, E])
        G = [sb(f"G{q}", [P, J, E, R]) for q in range(2)]
        GT = sb("GT", [P, NB, J * P])
        GT_now = [sb(f"GT_now{q}", [P, J, P]) for q in range(2)]

        ps_P = bank("ps_P", [P, BANKS, N])
        ps_X = [bank(f"ps_X{g}", [P, N]) for g in range(2)]
        ps_B = [bank(f"ps_B{q}", [P, N]) for q in range(2)]
        BX_AT = J * P
        ps_F = [ps_X, ps_B]
        BG_banks = (ps_P[:, 2, :], ps_P[:, 3, :], ps_B[1], ps_B[0])

        A_landed = sem("A_landed")
        B_landed = sem("B_landed")
        ids_landed = sem("ids_landed")
        gate_landed = sem("gate_landed")
        x_landed = [sem(f"x_landed{q}") for q in range(2)]
        W_landed = [sem(f"W_landed{n}") for n in range(4)]
        W_begun = sem("W_begun")
        zeroed = sem("zeroed")
        consts_made = sem("consts_made")
        A_turned = [sem(f"A_turned{half}") for half in range(2)]
        picks = sem("picks")
        gate_widened = sem("gate_widened")
        AG_T_done = sem("AG_T_done")
        AG_T_copied = sem("AG_T_copied")
        AG_done = sem("AG_done")
        BG_done = sem("BG_done")
        BG_copied = sem("BG_copied")
        xT_done = sem("xT_done")
        xT_copied = [sem(f"xT_copied{g}") for g in range(2)]
        BG_staged = sem("BG_staged")
        BxT_done = sem("BxT_done")
        BxT_copied = sem("BxT_copied")
        x_kept = sem("x_kept")
        Bx_done = sem("Bx_done")
        routed = sem("routed")
        exp_done = sem("exp_done")
        GT_done = sem("GT_done")
        GT_copied = sem("GT_copied")
        GT_staged = sem("GT_staged")
        W_used = sem("W_used")
        slots_freed = sem("slots_freed")
        odd_rows = sem("odd_rows")
        even_rows = sem("even_rows")
        last_wholes = sem("last_wholes")
        F_done = sem("F_done")
        F_added = sem("F_added")
        stored = [sem(f"stored{blk}") for blk in range(2)]

        block = ctx.enter_context(nc.Block())

        def whole(copy, pair, j, odd_adapter):
            blk, i = pair // PAIRS, pair % PAIRS
            n = (2 * pair + (0 if odd_adapter else 1)) % BANKS
            return copy(M_sb[Q * i:Q * i + Q, blk * NA + 2 * j + odd_adapter, :], ps_P[Q * j:Q * j + Q, n, :])

        def first_half(copy, pair, j, odd_adapter):
            blk, i = pair // PAIRS, pair % PAIRS
            n = (2 * pair + (1 if odd_adapter else 0)) % BANKS
            return copy(M_sb[Q * i:Q * i + R, blk * NA + 2 * j + odd_adapter, :], ps_P[Q * j:Q * j + R, n, :])

        def store_tile(engine, b, j):
            columns = slice(N, 2 * N)
            engine.dma_start(out_dram[:, b, j, columns], x_keep[:, b, j, columns]).then_inc(stored[1], DMA)

        def store(engine, b, blk):
            columns = slice(blk * N, (blk + 1) * N)
            engine.dma_start(out_dram[:, bass.ds(b, 1), :, columns].rearrange("p b j n -> p (b j) n"),
                             x_keep[:, bass.ds(b, 1), :, columns].rearrange("p b j n -> p (b j) n")
                             ).then_inc(stored[blk], DMA)

        def turn_A(copy, half, version):
            chunks = slice(half * HALF, (half + 1) * HALF)
            if version == 0:
                copy(A_T[0][:, chunks, :].rearrange("p k (a r) -> p k a r", a=NA),
                     A_sb[:].rearrange("p a (k r) -> p k a r", k=K)[:, chunks]).then_inc(A_turned[half], 1)
            else:
                swapped = A_T[1][:].rearrange("p k (j h r) -> p k j h r", h=2, r=R)
                given = A_sb[:].rearrange("p (j h) (k r) -> p k j h r", h=2, k=K)
                for h in range(2):
                    copy(swapped[:, chunks, :, h, :], given[:, chunks, :, 1 - h, :]).then_inc(A_turned[half], 1)

        @block.sync
        def _(sp):
            def place(trip, q):
                step = trip * 2 + q
                return step & (E - 1), ((step >> (E.bit_length() - 1)) & (BLOCKS - 1)) * N

            def load_W(e, column, q, half):
                n = 2 * q + half
                sp.dma_start(W_sb[n][:],
                             W_dram[:, bass.ds(e, 1), half * HALF:(half + 1) * HALF, bass.ds(column, N)]
                             .rearrange("p e k o -> p (e k) o")).then_inc(W_landed[n], DMA)

            def load_x(b, q):
                sp.dma_start(x_in[q][:], x_dram[:, bass.ds(b, 1)].rearrange("p b j i -> p (b j) i")
                             ).then_inc(x_landed[q], DMA)

            def load_ahead(trip, with_x):
                for q in range(2):
                    e, column = (sp.snap(v) for v in place(trip, q))
                    for half in range(2):
                        sp.wait_ge(W_used, trip * 4 + (2 * q + half - 3))
                        sp.sem_inc(slots_freed, 1)
                        load_W(e, column, q, half)
                    if with_x:
                        b = trip * 2 + q
                        sp.wait_ge(x_kept, b - 1)
                        sp.sem_inc(slots_freed, 1)
                        sp.wait_ge(xT_done, b * (2 * J) - 2 * J)
                        sp.sem_inc(slots_freed, 1)
                        load_x(b, q)

            sp.dma_start(A_sb[:], A_dram).then_inc(A_landed, DMA)
            sp.dma_start(W_sb[0][:, 0:BEGIN, :], W_dram[:, 0, 0:BEGIN, 0:N]).then_inc(W_begun, DMA)
            sp.dma_start(W_sb[0][:, BEGIN:, :], W_dram[:, 0, BEGIN:HALF, 0:N]).then_inc(W_landed[0], DMA)
            load_W(0, 0, 0, 1)
            sp.dma_start(B_sb[:], B.rearrange("a r i -> (a r) i")).then_inc(B_landed, DMA)
            load_x(0, 0)
            load_W(1, 0, 1, 0)
            load_W(1, 0, 1, 1)
            load_x(1, 1)
            with sp.Fori(1, PAIRS) as trip:
                load_ahead(trip, True)
            with sp.Fori(PAIRS, STEPS // 2) as trip:
                load_ahead(trip, False)

            for first, end, blk in ((NB - LAG - 2, NB, 0), (NB, 2 * NB - 2, 1)):
                with sp.Fori(first, end) as u:
                    sp.wait_ge(F_added, u * J + J)
                    sp.sem_inc(slots_freed, 1)
                    store(sp, u - blk * NB, blk)
            for b in range(NB - 2, NB):
                for j in range(J):
                    sp.wait_ge(F_added, (NB + b) * J + j + 1)
                    store_tile(sp, b, j)
            sp.wait_ge(stored[0], NB * DMA)
            sp.wait_ge(stored[1], (NB - 2 + 2 * J) * DMA)

        @block.gpsimd
        def _(pool):
            nc.gpsimd.memset(ident[:], 0.0).then_inc(zeroed, 1)
            pool.wait_ge(zeroed, 1)
            nc.gpsimd.affine_select(out=ident[:], in_=ident[:], compare_op=ALU.not_equal, fill=1.0, base=0,
                                    pattern=[[-1, P]], channel_multiplier=1).then_inc(consts_made, 1)
            nc.gpsimd.iota(row_no[:], pattern=[[0, 1]], base=0, channel_multiplier=1,
                           allow_small_or_imprecise_dtypes=True).then_inc(consts_made, 1)
            nc.gpsimd.iota(count_up[:], pattern=[[1, R]], base=0, channel_multiplier=0,
                           allow_small_or_imprecise_dtypes=True).then_inc(consts_made, 1)
            for half, value in enumerate((1.0, -1.0)):
                nc.gpsimd.memset(other[:].rearrange("p (i h) -> p i h", h=2)[:, :, half], value).then_inc(consts_made, 1)

            nc.gpsimd.memset(gate_wide[:], 0.0).then_inc(zeroed, 1)
            nc.gpsimd.memset(BG[:, :, :, RG:], 0.0).then_inc(zeroed, 1)
            pool.wait_ge(zeroed, 3)
            pool.wait_ge(gate_landed, DMA)
            nc.gpsimd.tensor_copy(gate_wide[:, :, 0:E], gate_sb[:]).then_inc(gate_widened, 1)

            def stage_BG(b, q):
                nc.gpsimd.tensor_copy(BG_now[q][:].rearrange("p c n -> p (c n)"),
                                      BG[:, bass.ds(b, 1), :, :].rearrange("p b c n -> p (b c n)")).then_inc(BG_staged, 1)

            def keep_x(trip, q):
                pool.wait_ge(x_landed[q], trip * DMA + DMA)
                nc.gpsimd.tensor_copy(x_keep[:, bass.ds(trip * 2 + q, 1), :, :].rearrange("p b j i -> p (b j) i"),
                                      x_in[q][:]).then_inc(x_kept, 1)

            pool.wait_ge(BG_copied, 2 * len(BG_banks))
            for q in range(2):
                stage_BG(q, q)
                keep_x(0, q)
            with pool.Fori(1, NB // 2) as trip:
                for q in range(2):
                    pool.wait_ge(BxT_done, trip * 2 + (q - 1))
                    stage_BG(trip * 2 + q, q)
                    keep_x(trip, q)

        @block.scalar
        def _(act):
            act.dma_start(gate_sb[:], gate_dram).then_inc(gate_landed, DMA)
            act.dma_start(ids_sb[:], ids.rearrange("(a b) -> a b", a=1).to_broadcast([P, NB])).then_inc(ids_landed, DMA)

            def copy_BG():
                for n, ps in enumerate(BG_banks):
                    act.wait_ge(BG_done, n + 1)
                    v = ps[:, 0:2 * (P + NB * E)].rearrange("p (c n) -> p c n", c=2)
                    nc.scalar.copy(BG[:, :, 2 * n:2 * n + 2, 0:R],
                                   v[:, :, 0:P].rearrange("p c (b r) -> p b c r", b=NB)).then_inc(BG_copied, 1)
                    nc.scalar.copy(BG[:, :, 2 * n:2 * n + 2, R:RG],
                                   v[:, :, P:].rearrange("p c (b e) -> p b c e", b=NB)).then_inc(BG_copied, 1)

            def copy_xT(b, j):
                act.wait_ge(xT_done, (b * J + j) * 2 + 1)
                nc.scalar.copy(xT[:, 0:CG, j * P:(j + 1) * P],
                               ps_X[0][:].rearrange("p (c t) -> p c t", c=CG)).then_inc(xT_copied[0], 1)

            def odd_adapters(pair, part):
                if part is whole:
                    act.wait_ge(W_used, 4 * pair + 4)
                else:
                    act.wait_ge(odd_rows, 2 * pair + 1)
                    act.wait_ge(even_rows, 2 * pair + 1)
                for j in range(PAIRS):
                    last = part(nc.scalar.copy, pair, j, 1)
                last.then_inc(odd_rows, 1)

            def odd_adapters_after(step):
                if step >= 1:
                    odd_adapters((step - 1) // 2, whole if step % 2 else first_half)

            def copy_GT(b):
                act.wait_ge(GT_done, b + 1)
                nc.scalar.copy(GT[:, b, :], ps_B[b % 2][:, 0:J * P]).then_inc(GT_copied, 1)

            def exps(b):
                act.wait_ge(routed, b * ROUTE_OPS + GAP_OP)
                nc.scalar.activation(exp_gap[:], gap[:], ACT.Exp).then_inc(exp_done, 1)

            def copy_BxT(b):
                act.wait_ge(BxT_done, b + 1)
                nc.scalar.copy(BxT[:], ps_B[b % 2][:, 0:J * P]).then_inc(BxT_copied, 1)

            def stage_GT(u):
                if u >= 2:
                    act.wait_ge(F_done, (u - 1) * J)
                nc.scalar.copy(GT_now[u % 2][:].rearrange("p j t -> p (j t)"), GT[:, u % NB, :]).then_inc(GT_staged, 1)

            act.wait_ge(A_landed, DMA)
            turn_A(nc.scalar.copy, 1, 0)
            turn_A(nc.scalar.copy, 1, 1)
            act.wait_ge(AG_T_done, 1)
            nc.scalar.copy(AG_T[:], ps_B[1][:, 0:P]).then_inc(AG_T_copied, 1)
            copy_BG()
            for b in range(NB):
                if b:
                    copy_BxT(b - 1)
                copy_xT(b, 0)
                if b:
                    exps(b - 1)
                odd_adapters_after(b)
                copy_xT(b, 1)
                if b:
                    copy_GT(b - 1)
            copy_BxT(NB - 1)
            odd_adapters_after(E)
            exps(NB - 1)
            for step in range(E + 1, STEPS - 1):
                odd_adapters_after(step)
                if step == E + 1:
                    copy_GT(NB - 1)
                    act.wait_ge(GT_copied, NB)
                u = step - E - LAG
                if u + 1 >= 0:
                    stage_GT(u + 1)
                if u - 1 >= 0:
                    act.wait_ge(F_added, u * J)
                    store(act, u - 1, 0)
            pair = STEPS // 2 - 1
            act.wait_ge(W_used, 4 * pair + 2)
            for j in range(PAIRS):
                last = whole(nc.scalar.copy, pair, j, 1)
            last.then_inc(odd_rows, 1)
            stage_GT(NB - LAG)
            act.wait_ge(W_used, 4 * pair + 4)
            for j in range(1, PAIRS):
                whole(nc.scalar.copy, pair, j, 0).then_inc(last_wholes, 1)
            act.wait_ge(odd_rows, 2 * pair + 1)
            for j in range(1, PAIRS):
                first_half(nc.scalar.copy, pair, j, 1)
            stage_GT(NB - LAG + 1)
            act.wait_ge(last_wholes, PAIRS - 1)
            for j in range(2, PAIRS):
                last = first_half(nc.scalar.copy, pair, j, 0)
            last.then_inc(odd_rows, 1)
            for u in range(NB, 2 * NB):
                stage_GT(u)

        @block.vector
        def _(dve):
            done = [0]

            def pick_step(ins):
                done[0] += 1
                ins.then_inc(picks, 1)
                dve.wait_ge(picks, done[0])

            dve.wait_ge(A_landed, DMA)
            for version in range(2):
                turn_A(nc.vector.tensor_copy, 0, version)

            dve.wait_ge(consts_made, 5)
            dve.wait_ge(ids_landed, DMA)
            pick_step(nc.vector.tensor_copy(ids_f[:], ids_sb[:]))
            pick_step(nc.vector.tensor_scalar(row_of[:], ids_f[:], float(-R), row_no[:, 0:1], ALU.mult, ALU.add))
            pick_r = pick[:, 0:NB * R].rearrange("p (b r) -> p b r", b=NB)
            pick_step(nc.vector.tensor_tensor(pick_r, row_of[:].unsqueeze(2).to_broadcast([P, NB, R]),
                                              count_up[:].unsqueeze(1).to_broadcast([P, NB, R]), ALU.is_equal))
            pick_step(nc.vector.tensor_reduce(picked[:], pick_r, AX_X, ALU.add))
            dve.wait_ge(AG_done, 1)
            parts = ps_B[0][:, 0:P].rearrange("p (n m) -> p m n", n=QUADS)
            pick_step(nc.vector.tensor_reduce(AG[:], parts[:, 0:E, :], AX_X, ALU.add))
            pick_step(nc.vector.tensor_tensor(pick[:, NB * R:].rearrange("p (b e) -> p b e", b=NB),
                                              AG[:].unsqueeze(1).to_broadcast([P, NB, E]),
                                              picked[:].unsqueeze(2).to_broadcast([P, NB, E]), ALU.mult))
            assert done[0] == PICK_STEPS
            pick_step(nc.vector.tensor_scalar(odd_i[:], ids_sb[:], 1, None, ALU.bitwise_and))
            pick_step(nc.vector.tensor_copy(odd_f[:], odd_i[:]))
            pick_step(nc.vector.tensor_tensor(slot_expert[:], odd_f[:].unsqueeze(2).to_broadcast([P, NB, E]),
                                              other[:].unsqueeze(1).to_broadcast([P, NB, E]), ALU.mult))
            pick_step(nc.vector.tensor_tensor(slot_expert[:], slot_expert[:],
                                              count_up[:, 0:E].unsqueeze(1).to_broadcast([P, NB, E]), ALU.add))

            def copy_xT(b, j):
                dve.wait_ge(xT_done, (b * J + j) * 2 + 2)
                nc.vector.tensor_copy(xT[:, CG:, j * P:(j + 1) * P],
                                      ps_X[1][:].rearrange("p (c t) -> p c t", c=CG)).then_inc(xT_copied[1], 1)

            def route(b):
                q = b % 2
                n = [0]

                def step(ins):
                    n[0] += 1
                    ins.then_inc(routed, 1)

                def steps_done():
                    dve.wait_ge(routed, b * ROUTE_OPS + n[0])

                dve.wait_ge(Bx_done, b + 1)
                parts = ps_B[q][:, BX_AT:].rearrange("p (j n m) -> p j m n", j=J, n=QUADS)
                step(nc.vector.tensor_reduce(Bx[q][:], parts[:, :, 0:RG, :], AX_X, ALU.add))
                steps_done()
                step(nc.vector.memset(total[:], 1.0))
                for j in range(J):
                    step(nc.vector.max(top[:, j, :], Bx[q][:, j, R:RG]))
                steps_done()
                step(nc.vector.tensor_tensor(gap[:], top[:, :, 1], top[:, :, 0], ALU.subtract))
                for j in range(J):
                    step(nc.vector.max_index(top_no[:, j, :], top[:, j, :], Bx[q][:, j, R:RG]))
                steps_done()
                step(nc.vector.tensor_copy(top_nof[:], top_no[:, :, 0:TOP]))
                steps_done()
                hot_jk = hot[:].rearrange("p j k e -> p (j k) e")
                step(nc.vector.tensor_tensor(hot_jk,
                                             slot_expert[:, b, :].unsqueeze(1).to_broadcast([P, J * TOP, E]),
                                             top_nof[:].rearrange("p j k -> p (j k)").unsqueeze(2)
                                             .to_broadcast([P, J * TOP, E]), ALU.is_equal))
                dve.wait_ge(exp_done, b + 1)
                step(nc.vector.tensor_tensor(total[:], total[:], exp_gap[:], ALU.add))
                steps_done()
                step(nc.vector.reciprocal(prob[:, :, 0], total[:]))
                steps_done()
                step(nc.vector.tensor_tensor(prob[:, :, 1], prob[:, :, 0], exp_gap[:], ALU.mult))
                steps_done()
                step(nc.vector.tensor_tensor(hot_jk, hot_jk, prob[:].rearrange("p j k -> p (j k)").unsqueeze(2)
                                             .to_broadcast([P, J * TOP, E]), ALU.mult))
                steps_done()
                step(nc.vector.tensor_tensor(w_e[:], hot[:, :, 0, :], hot[:, :, 1, :], ALU.add))
                steps_done()
                for j in range(J):
                    last = nc.vector.tensor_tensor(G[q][:, j, :, :],
                                                   Bx[q][:, j, 0:R].unsqueeze(1).to_broadcast([P, E, R]),
                                                   w_e[:, j, :].unsqueeze(2).to_broadcast([P, E, R]), ALU.mult)
                step(last)
                assert n[0] == ROUTE_OPS

            def even_adapters(pair, part):
                if part is whole:
                    dve.wait_ge(W_used, 4 * pair + 4)
                else:
                    dve.wait_ge(even_rows, 2 * pair + 1)
                    dve.wait_ge(odd_rows, 2 * pair + 1)
                for j in range(PAIRS):
                    last = part(nc.vector.tensor_copy, pair, j, 0)
                last.then_inc(even_rows, 1)

            def even_adapters_after(step):
                if step >= 1:
                    even_adapters((step - 1) // 2, whole if step % 2 else first_half)

            def add(u, q, blk):
                b = u - blk * NB
                for j in range(J):
                    dve.wait_ge(F_done, u * J + (j + 1))
                    v = x_keep[:, bass.ds(b, 1), j, blk * N:(blk + 1) * N].rearrange("p b n -> p (b n)")
                    nc.vector.tensor_tensor(v, v, ps_F[q][j][:], ALU.add).then_inc(F_added, 1)

            for b in range(NB):
                copy_xT(b, 0)
                if b:
                    route(b - 1)
                even_adapters_after(b)
                copy_xT(b, 1)
            even_adapters_after(E)
            route(NB - 1)
            dve.wait_ge(x_kept, NB)
            for step in range(E + 1, STEPS - 1):
                even_adapters_after(step)
                if step - E >= LAG:
                    add(step - E - LAG, step % 2, 0)
            last_pair = STEPS // 2 - 1
            dve.wait_ge(W_used, 2 * STEPS)
            whole(nc.vector.tensor_copy, last_pair, 0, 0).then_inc(even_rows, 1)
            dve.wait_ge(odd_rows, 2 * last_pair + 1)
            first_half(nc.vector.tensor_copy, last_pair, 0, 1)
            dve.wait_ge(last_wholes, 1)
            dve.wait_ge(even_rows, 2 * last_pair + 1)
            for j in range(2):
                last = first_half(nc.vector.tensor_copy, last_pair, j, 0)
            last.then_inc(even_rows, 1)
            add(NB - LAG - 1, (NB - LAG - 1) % 2, 0)
            for u in range(NB - LAG, NB):
                add(u, u % 2, 0)
            with dve.Fori(PAIRS, 2 * PAIRS) as trip:
                for q in range(2):
                    add(trip * 2 + q, q, 1)

        @block.tensor
        def _(pe):
            def experts_product(trip, q, half, waits):
                step = trip * 2 + q
                n = 2 * q + half
                out_bank = ps_P[:, bass.ds((trip & 1) * 2 + q, 1), :].rearrange("p b n -> p (b n)")
                if waits and (q, half) == (0, 0):
                    pe.wait_ge(odd_rows, trip * 2 - 2)
                    pe.wait_ge(even_rows, trip * 2 - 2)
                first = isinstance(step, int) and step == 0 and half == 0
                if not first:
                    pe.wait_ge(W_landed[n], trip * DMA + DMA)
                for k in range(HALF):
                    if first and k == BEGIN:
                        pe.wait_ge(W_landed[n], DMA)
                    kk = half * HALF + k
                    last = nc.tensor.matmul(out_bank, A_T[q][:, kk, :], W_sb[n][:, k, :],
                                            start=(kk == 0), stop=(kk == K - 1))
                last.then_inc(W_used, 1)

            def x_transposes(trip, q, j):
                b = trip * 2 + q
                if j == 0:
                    pe.wait_ge(x_landed[q], trip * DMA + DMA)
                for g in range(2):
                    if not (isinstance(b, int) and b == 0 and j == 0):
                        pe.wait_ge(xT_copied[g], b * J + j)
                    for c in range(CG):
                        cc = g * CG + c
                        last = nc.tensor.transpose(ps_X[g][:, c * P:(c + 1) * P],
                                                   x_in[q][:, j, cc * P:(cc + 1) * P], ident[:])
                    last.then_inc(xT_done, 1)

            def BxT_product(trip, q):
                b = trip * 2 + q
                pe.wait_ge(BG_staged, b + 1)
                for g in range(2):
                    pe.wait_ge(xT_copied[g], b * J + J)
                if not (isinstance(trip, int) and trip == 0):
                    pe.wait_ge(GT_copied, b - 1)
                for c in range(C):
                    n = c % QUADS
                    last = nc.tensor.matmul(ps_B[q][n * Q:(n + 1) * Q, 0:J * P], BG_now[q][:, c, :], xT[:, c, :],
                                            start=(c < QUADS), stop=(c >= C - QUADS), tile_position=(0, n * Q))
                last.then_inc(BxT_done, 1)

            def Bx_transposes(b, q):
                pe.wait_ge(BxT_copied, b + 1)
                for j in range(J):
                    last = nc.tensor.transpose(ps_B[q][:, BX_AT + j * P:BX_AT + (j + 1) * P],
                                               BxT[:, j * P:(j + 1) * P], ident[:])
                last.then_inc(Bx_done, 1)

            def g_transposes(b, q):
                pe.wait_ge(routed, b * ROUTE_OPS + ROUTE_OPS)
                for j in range(J):
                    last = nc.tensor.transpose(ps_B[q][:, j * P:(j + 1) * P],
                                               G[q][:, j, :, :].rearrange("p e r -> p (e r)"), ident[:])
                last.then_inc(GT_done, 1)

            def x_step(trip, q, first):
                experts = (trip, 1) if q == 0 else (trip + 1, 0)
                x_transposes(trip, q, 0)
                if not first:
                    Bx_transposes(trip * 2 + (q - 1), 1 - q)
                experts_product(*experts, 0, not (isinstance(trip, int) and trip == 0))
                x_transposes(trip, q, 1)
                experts_product(*experts, 1, False)
                if not first:
                    g_transposes(trip * 2 + (q - 1), 1 - q)
                BxT_product(trip, q)

            def final(trip, q, blk, waits):
                u = trip * 2 + q
                a = pe.value_load(ids_sb[0:1, bass.ds(u - blk * NB, 1)], min_val=0, max_val=NA - 1)
                pe.wait_ge(GT_staged, u + 1)
                for j in range(J):
                    if waits:
                        pe.wait_ge(F_added, u * J + (j + 1 - 2 * J))
                    nc.tensor.matmul(ps_F[q][j][:], GT_now[q][:, j, :],
                                     M_sb[:, bass.ds(a + blk * NA, 1), :].rearrange("p b n -> p (b n)"),
                                     start=True, stop=True).then_inc(F_done, 1)

            def warm(products):
                for _ in range(products):
                    nc.tensor.matmul(ps_X[0][:, 0:P], ident[:], ident[:], start=True, stop=True)

            pe.wait_ge(consts_made, 5)
            warm(WARM_UP)
            pe.wait_ge(gate_widened, 1)
            for k in range(K):
                if k % HALF == 0:
                    pe.wait_ge(A_turned[k // HALF], 1)
                n = k % QUADS
                last = nc.tensor.matmul(ps_B[1][n * Q:(n + 1) * Q, 0:P], gate_wide[:, k, :], A_T[0][:, k, :],
                                        start=(k < QUADS), stop=(k >= K - QUADS), tile_position=(0, n * Q))
            last.then_inc(AG_T_done, 1)
            warm(KEEP_WARM)
            pe.wait_ge(AG_T_copied, 1)
            nc.tensor.transpose(ps_B[0][:, 0:P], AG_T[:], ident[:]).then_inc(AG_done, 1)
            pe.wait_ge(W_begun, DMA)
            for half in range(2):
                experts_product(0, 0, half, False)
            pe.wait_ge(B_landed, DMA)
            pe.wait_ge(picks, PICK_STEPS)
            for n, ps in enumerate(BG_banks):
                for c in range(2):
                    at = c * (P + NB * E)
                    last = nc.tensor.matmul(ps[:, at:at + P + NB * E], B_sb[:, (2 * n + c) * P:(2 * n + c + 1) * P],
                                            pick[:], start=True, stop=True)
                last.then_inc(BG_done, 1)


            for half in range(2):
                pe.wait_ge(A_turned[half], 3)
            for q in range(2):
                x_step(0, q, q == 0)
            with pe.Fori(1, PAIRS) as trip:
                for q in range(2):
                    x_step(trip, q, False)

            experts_product(PAIRS, 1, 0, True)
            Bx_transposes(NB - 1, 1)
            experts_product(PAIRS, 1, 1, True)

            def block1_trip(trip, final_waits):
                for q in range(2):
                    experts_product(trip, q, 0, True)
                    if not final_waits and q == 0:
                        g_transposes(NB - 1, 1)
                    experts_product(trip, q, 1, True)
                    final(trip - (PAIRS + LAG // 2), q, 0, final_waits)

            pe.wait_ge(ids_landed, DMA)
            block1_trip(PAIRS + 1, False)
            with pe.Fori(PAIRS + 2, 2 * PAIRS) as trip:
                block1_trip(trip, True)
            for q in range(2):
                final(PAIRS - 1, q, 0, True)
            pe.wait_ge(odd_rows, STEPS)
            pe.wait_ge(even_rows, STEPS)
            for q in range(2):
                final(PAIRS, q, 1, True)
            with pe.Fori(PAIRS + 1, 2 * PAIRS) as trip:
                for q in range(2):
                    final(trip, q, 1, True)


def kernel(x, itok_B_3_7, L0_cond_A, L0_cond_B, L0_ffn_gate_w, L0_ffn_expert_w):
    import numpy as np
    import concourse.bacc as bacc
    from concourse.bass_utils import run_bass_kernel_spmd

    nc = bacc.Bacc("TRN2", target_bir_lowering=False, num_devices=1)
    given = {"x": x, "ids": itok_B_3_7, "A": L0_cond_A, "B": L0_cond_B, "gate_w": L0_ffn_gate_w,
             "W": L0_ffn_expert_w}
    arrays, args = {}, []
    for name, a in given.items():
        a = np.ascontiguousarray(a)
        arrays[f"{name}_dram"] = a
        args.append(nc.dram_tensor(f"{name}_dram", a.shape, mybir.dt.from_np(a.dtype), kind="ExternalInput").ap())
    result = nc.dram_tensor("out_dram", arrays["x_dram"].shape, F32, kind="ExternalOutput").ap()
    adaln_ffn(nc, *args, result)
    r = run_bass_kernel_spmd(nc, [arrays], core_ids=[0])
    return r.results[0]["out_dram"]
```

```python
from contextlib import ExitStack

import concourse.bass as bass
from concourse import mybir


P = 128
Q = 32
F32 = mybir.dt.float32
I32 = mybir.dt.int32
U32 = mybir.dt.uint32
ALU = mybir.AluOpType
ACT = mybir.ActivationFunctionType
AX_X = mybir.AxisListType.X
TOP = 2
LANES8 = 8
DMA = 16
ROUTE_OPS = 15
GAP_OP = 5
AG_STEPS = 2
LAG = 2
BEGIN = 2
WARM_UP = 7
KEEP_WARM = 2


def adaln_ffn(nc, x, ids, A, B, gate_w, W, out):
    NB, S, D = x.shape
    NA, H, R = A.shape
    E, _, O = W.shape
    J = S // P
    C = D // P
    CG = C // 2
    K = H // P
    HALF = K // 2
    N = 512
    BLOCKS = O // N
    PAIRS = E // 2
    STEPS = BLOCKS * E
    RG = R + E
    BANKS = 4
    QUADS = P // Q
    assert RG <= Q and C % QUADS == 0
    assert NA * R == P and E * R == P and 2 * R == Q and NB == E and E == LANES8 and J == 2 and BLOCKS == 2

    x_dram = x.rearrange("b (p j) i -> p b j i", j=J)
    out_dram = out.rearrange("b (p j) o -> p b j o", j=J)
    A_dram = A.rearrange("a (p k) r -> p a (k r)", k=K)
    W_dram = W.rearrange("e (p k) o -> p e k o", k=K)
    gate_dram = gate_w.rearrange("(p k) e -> p k e", k=K)

    with ExitStack() as ctx:
        def sb(name, shape, dt=F32):
            return ctx.enter_context(nc.sbuf_tensor(name, shape, dt))

        def bank(name, shape):
            return ctx.enter_context(nc.psum_tensor(name, shape, F32))

        def sem(name):
            return ctx.enter_context(nc.semaphore(name))

        ids_sb = sb("ids_sb", [P, NB], I32)
        odd_i = sb("odd_i", [P, NB], I32)
        odd_f = sb("odd_f", [P, NB])
        ident = sb("ident", [P, P])
        count_up = sb("count_up", [P, R])
        other = sb("other", [P, E])
        own = sb("own", [P, NA])
        AG_own = sb("AG_own", [P, NA, E])
        slot_expert = sb("slot_expert", [P, NB, E])
        A_sb = sb("A_sb", [P, NA, K * R])
        A_T = [sb(f"A_T{v}", [P, K, P]) for v in range(2)]
        B_sb = sb("B_sb", [P, D])
        gate_sb = sb("gate_sb", [P, K, E])
        gate_wide = sb("gate_wide", [P, K, Q])
        AG = sb("AG", [P, E])
        AG_T = sb("AG_T", [P, P])
        BG = sb("BG", [P, NA, C, Q])
        BG_now = [sb(f"BG_now{q}", [P, C, Q]) for q in range(2)]
        W_sb = [sb(f"W_sb{n}", [P, HALF, N]) for n in range(4)]
        M_sb = sb("M_sb", [P, BLOCKS * NA, N])
        x_in = [sb(f"x_in{q}", [P, J, D]) for q in range(2)]
        x_keep = sb("x_keep", [P, NB, J, D])
        xT = sb("xT", [P, C, J * P])
        BxT = sb("BxT", [P, J * P])
        Bx = [sb(f"Bx{q}", [P, J, RG]) for q in range(2)]
        top = sb("top", [P, J, LANES8])
        top_no = sb("top_no", [P, J, LANES8], U32)
        top_nof = sb("top_nof", [P, J, TOP])
        gap = sb("gap", [P, J])
        exp_gap = sb("exp_gap", [P, J])
        total = sb("total", [P, J])
        prob = sb("prob", [P, J, TOP])
        hot = sb("hot", [P, J, TOP, E])
        w_e = sb("w_e", [P, J, E])
        G = [sb(f"G{q}", [P, J, E, R]) for q in range(2)]
        GT = sb("GT", [P, NB, J * P])
        GT_now = [sb(f"GT_now{q}", [P, J, P]) for q in range(2)]

        ps_P = bank("ps_P", [P, BANKS, N])
        ps_X = [bank(f"ps_X{g}", [P, N]) for g in range(2)]
        ps_B = [bank(f"ps_B{q}", [P, N]) for q in range(2)]
        BX_AT = J * P
        ps_F = [ps_X, ps_B]
        BG_banks = (ps_P[:, 2, :], ps_P[:, 3, :], ps_B[1], ps_B[0])

        A_landed = sem("A_landed")
        B_landed = sem("B_landed")
        ids_landed = sem("ids_landed")
        gate_landed = sem("gate_landed")
        x_landed = [sem(f"x_landed{q}") for q in range(2)]
        W_landed = [sem(f"W_landed{n}") for n in range(4)]
        W_begun = sem("W_begun")
        zeroed = sem("zeroed")
        own_steps = sem("own_steps")
        consts_made = sem("consts_made")
        A_turned = [sem(f"A_turned{half}") for half in range(2)]
        tables = sem("tables")
        gate_widened = sem("gate_widened")
        AG_T_done = sem("AG_T_done")
        AG_T_copied = sem("AG_T_copied")
        AG_done = sem("AG_done")
        BG_done = sem("BG_done")
        BG_copied = sem("BG_copied")
        xT_done = sem("xT_done")
        xT_copied = [sem(f"xT_copied{g}") for g in range(2)]
        BG_staged = sem("BG_staged")
        BxT_done = sem("BxT_done")
        BxT_copied = sem("BxT_copied")
        x_kept = sem("x_kept")
        Bx_done = sem("Bx_done")
        routed = sem("routed")
        exp_done = sem("exp_done")
        GT_done = sem("GT_done")
        GT_copied = sem("GT_copied")
        GT_staged = sem("GT_staged")
        W_used = sem("W_used")
        slots_freed = sem("slots_freed")
        odd_rows = sem("odd_rows")
        even_rows = sem("even_rows")
        last_wholes = sem("last_wholes")
        F_done = sem("F_done")
        F_added = sem("F_added")
        stored = [sem(f"stored{blk}") for blk in range(2)]

        block = ctx.enter_context(nc.Block())

        def whole(copy, pair, j, odd_adapter):
            blk, i = pair // PAIRS, pair % PAIRS
            n = (2 * pair + (0 if odd_adapter else 1)) % BANKS
            return copy(M_sb[Q * i:Q * i + Q, blk * NA + 2 * j + odd_adapter, :], ps_P[Q * j:Q * j + Q, n, :])

        def first_half(copy, pair, j, odd_adapter):
            blk, i = pair // PAIRS, pair % PAIRS
            n = (2 * pair + (1 if odd_adapter else 0)) % BANKS
            return copy(M_sb[Q * i:Q * i + R, blk * NA + 2 * j + odd_adapter, :], ps_P[Q * j:Q * j + R, n, :])

        def store_tile(engine, b, j):
            columns = slice(N, 2 * N)
            engine.dma_start(out_dram[:, b, j, columns], x_keep[:, b, j, columns]).then_inc(stored[1], DMA)

        def store(engine, b, blk):
            columns = slice(blk * N, (blk + 1) * N)
            engine.dma_start(out_dram[:, bass.ds(b, 1), :, columns].rearrange("p b j n -> p (b j) n"),
                             x_keep[:, bass.ds(b, 1), :, columns].rearrange("p b j n -> p (b j) n")
                             ).then_inc(stored[blk], DMA)

        def turn_A(copy, half, version):
            chunks = slice(half * HALF, (half + 1) * HALF)
            if version == 0:
                copy(A_T[0][:, chunks, :].rearrange("p k (a r) -> p k a r", a=NA),
                     A_sb[:].rearrange("p a (k r) -> p k a r", k=K)[:, chunks]).then_inc(A_turned[half], 1)
            else:
                swapped = A_T[1][:].rearrange("p k (j h r) -> p k j h r", h=2, r=R)
                given = A_sb[:].rearrange("p (j h) (k r) -> p k j h r", h=2, k=K)
                for h in range(2):
                    copy(swapped[:, chunks, :, h, :], given[:, chunks, :, 1 - h, :]).then_inc(A_turned[half], 1)

        @block.sync
        def _(sp):
            def place(trip, q):
                step = trip * 2 + q
                return step & (E - 1), ((step >> (E.bit_length() - 1)) & (BLOCKS - 1)) * N

            def load_W(e, column, q, half):
                n = 2 * q + half
                sp.dma_start(W_sb[n][:],
                             W_dram[:, bass.ds(e, 1), half * HALF:(half + 1) * HALF, bass.ds(column, N)]
                             .rearrange("p e k o -> p (e k) o")).then_inc(W_landed[n], DMA)

            def load_x(b, q):
                sp.dma_start(x_in[q][:], x_dram[:, bass.ds(b, 1)].rearrange("p b j i -> p (b j) i")
                             ).then_inc(x_landed[q], DMA)

            def load_ahead(trip, with_x):
                for q in range(2):
                    e, column = (sp.snap(v) for v in place(trip, q))
                    for half in range(2):
                        sp.wait_ge(W_used, trip * 4 + (2 * q + half - 3))
                        sp.sem_inc(slots_freed, 1)
                        load_W(e, column, q, half)
                    if with_x:
                        b = trip * 2 + q
                        sp.wait_ge(x_kept, b - 1)
                        sp.sem_inc(slots_freed, 1)
                        sp.wait_ge(xT_done, b * (2 * J) - 2 * J)
                        sp.sem_inc(slots_freed, 1)
                        load_x(b, q)

            sp.dma_start(A_sb[:], A_dram).then_inc(A_landed, DMA)
            sp.dma_start(W_sb[0][:, 0:BEGIN, :], W_dram[:, 0, 0:BEGIN, 0:N]).then_inc(W_begun, DMA)
            sp.dma_start(W_sb[0][:, BEGIN:, :], W_dram[:, 0, BEGIN:HALF, 0:N]).then_inc(W_landed[0], DMA)
            load_W(0, 0, 0, 1)
            sp.dma_start(B_sb[:], B.rearrange("a r i -> (a r) i")).then_inc(B_landed, DMA)
            load_W(1, 0, 1, 0)
            load_x(0, 0)
            load_W(1, 0, 1, 1)
            load_x(1, 1)
            with sp.Fori(1, PAIRS) as trip:
                load_ahead(trip, True)
            with sp.Fori(PAIRS, STEPS // 2) as trip:
                load_ahead(trip, False)

            for first, end, blk in ((NB - LAG - 2, NB, 0), (NB, 2 * NB - 2, 1)):
                with sp.Fori(first, end) as u:
                    sp.wait_ge(F_added, u * J + J)
                    sp.sem_inc(slots_freed, 1)
                    store(sp, u - blk * NB, blk)
            for b in range(NB - 2, NB):
                for j in range(J):
                    sp.wait_ge(F_added, (NB + b) * J + j + 1)
                    store_tile(sp, b, j)
            sp.wait_ge(stored[0], NB * DMA)
            sp.wait_ge(stored[1], (NB - 2 + 2 * J) * DMA)

        @block.gpsimd
        def _(pool):
            nc.gpsimd.memset(ident[:], 0.0).then_inc(zeroed, 1)
            pool.wait_ge(zeroed, 1)
            nc.gpsimd.affine_select(out=ident[:], in_=ident[:], compare_op=ALU.not_equal, fill=1.0, base=0,
                                    pattern=[[-1, P]], channel_multiplier=1).then_inc(consts_made, 1)
            nc.gpsimd.iota(count_up[:], pattern=[[1, R]], base=0, channel_multiplier=0,
                           allow_small_or_imprecise_dtypes=True).then_inc(consts_made, 1)
            for half, value in enumerate((1.0, -1.0)):
                nc.gpsimd.memset(other[:].rearrange("p (i h) -> p i h", h=2)[:, :, half], value).then_inc(consts_made, 1)

            nc.gpsimd.memset(own[:], 1.0).then_inc(own_steps, 1)
            pool.wait_ge(own_steps, 1)
            nc.gpsimd.affine_select(out=own[:], in_=own[:], compare_op=ALU.is_ge, fill=0.0, base=0,
                                    pattern=[[-R, NA]], channel_multiplier=1).then_inc(own_steps, 1)
            pool.wait_ge(own_steps, 2)
            nc.gpsimd.affine_select(out=own[:], in_=own[:], compare_op=ALU.is_ge, fill=0.0, base=R - 1,
                                    pattern=[[R, NA]], channel_multiplier=-1).then_inc(own_steps, 1)

            nc.gpsimd.memset(gate_wide[:], 0.0).then_inc(zeroed, 1)
            nc.gpsimd.memset(BG[:, :, :, RG:], 0.0).then_inc(zeroed, 1)
            pool.wait_ge(zeroed, 3)
            pool.wait_ge(gate_landed, DMA)
            nc.gpsimd.tensor_copy(gate_wide[:, :, 0:E], gate_sb[:]).then_inc(gate_widened, 1)

            def stage_BG(b, q):
                a = pool.value_load(ids_sb[0:1, bass.ds(b, 1)], min_val=0, max_val=NA - 1)
                nc.gpsimd.tensor_copy(BG_now[q][:].rearrange("p c n -> p (c n)"),
                                      BG[:, bass.ds(a, 1), :, :].rearrange("p b c n -> p (b c n)")).then_inc(BG_staged, 1)

            pool.wait_ge(ids_landed, DMA)
            pool.wait_ge(BG_copied, 2 * len(BG_banks))
            for q in range(2):
                stage_BG(q, q)
            with pool.Fori(1, NB // 2) as trip:
                for q in range(2):
                    pool.wait_ge(BxT_done, trip * (2 * QUADS) + (q - 1) * QUADS)
                    stage_BG(trip * 2 + q, q)

        @block.scalar
        def _(act):
            act.dma_start(gate_sb[:], gate_dram).then_inc(gate_landed, DMA)
            act.dma_start(ids_sb[:], ids.rearrange("(a b) -> a b", a=1).to_broadcast([P, NB])).then_inc(ids_landed, DMA)

            def copy_BG():
                for n, ps in enumerate(BG_banks):
                    act.wait_ge(BG_done, n + 1)
                    v = ps[:, 0:2 * (P + NA * E)].rearrange("p (c n) -> p c n", c=2)
                    nc.scalar.copy(BG[:, :, 2 * n:2 * n + 2, 0:R],
                                   v[:, :, 0:P].rearrange("p c (a r) -> p a c r", a=NA)).then_inc(BG_copied, 1)
                    nc.scalar.copy(BG[:, :, 2 * n:2 * n + 2, R:RG],
                                   v[:, :, P:].rearrange("p c (a e) -> p a c e", a=NA)).then_inc(BG_copied, 1)

            def copy_xT(b, j):
                act.wait_ge(xT_done, (b * J + j) * 2 + 1)
                nc.scalar.copy(xT[:, 0:CG, j * P:(j + 1) * P],
                               ps_X[0][:].rearrange("p (c t) -> p c t", c=CG)).then_inc(xT_copied[0], 1)

            def odd_adapters(pair, part):
                if part is whole:
                    act.wait_ge(W_used, 4 * pair + 4)
                else:
                    act.wait_ge(odd_rows, 2 * pair + 1)
                    act.wait_ge(even_rows, 2 * pair + 1)
                for j in range(PAIRS):
                    last = part(nc.scalar.copy, pair, j, 1)
                last.then_inc(odd_rows, 1)

            def odd_adapters_after(step):
                if step >= 1:
                    odd_adapters((step - 1) // 2, whole if step % 2 else first_half)

            def copy_GT(b):
                act.wait_ge(GT_done, b + 1)
                nc.scalar.copy(GT[:, b, :], ps_B[b % 2][:, 0:J * P]).then_inc(GT_copied, 1)

            def exps(b):
                act.wait_ge(routed, b * ROUTE_OPS + GAP_OP)
                nc.scalar.activation(exp_gap[:], gap[:], ACT.Exp).then_inc(exp_done, 1)

            def keep_x(b):
                act.wait_ge(x_landed[b % 2], (b // 2 + 1) * DMA)
                nc.scalar.copy(x_keep[:, b, :, :], x_in[b % 2][:]).then_inc(x_kept, 1)

            def copy_BxT(b):
                act.wait_ge(BxT_done, b * QUADS + QUADS)
                nc.scalar.copy(BxT[:], ps_B[b % 2][:, 0:J * P]).then_inc(BxT_copied, 1)

            def stage_GT(u):
                if u >= 2:
                    act.wait_ge(F_done, (u - 1) * J)
                nc.scalar.copy(GT_now[u % 2][:].rearrange("p j t -> p (j t)"), GT[:, u % NB, :]).then_inc(GT_staged, 1)

            act.wait_ge(A_landed, DMA)
            turn_A(nc.scalar.copy, 1, 0)
            turn_A(nc.scalar.copy, 1, 1)
            act.wait_ge(AG_T_done, QUADS)
            nc.scalar.copy(AG_T[:], ps_B[1][:, 0:P]).then_inc(AG_T_copied, 1)
            copy_BG()
            for b in range(NB):
                if b:
                    copy_BxT(b - 1)
                copy_xT(b, 0)
                if b:
                    exps(b - 1)
                odd_adapters_after(b)
                copy_xT(b, 1)
                keep_x(b)
                if b:
                    copy_GT(b - 1)
            copy_BxT(NB - 1)
            odd_adapters_after(E)
            exps(NB - 1)
            for step in range(E + 1, STEPS - 1):
                odd_adapters_after(step)
                if step == E + 1:
                    copy_GT(NB - 1)
                    act.wait_ge(GT_copied, NB)
                u = step - E - LAG
                if u + 1 >= 0:
                    stage_GT(u + 1)
                if u - 1 >= 0:
                    act.wait_ge(F_added, u * J)
                    store(act, u - 1, 0)
            pair = STEPS // 2 - 1
            act.wait_ge(W_used, 4 * pair + 2)
            for j in range(PAIRS):
                last = whole(nc.scalar.copy, pair, j, 1)
            last.then_inc(odd_rows, 1)
            stage_GT(NB - LAG)
            act.wait_ge(W_used, 4 * pair + 4)
            for j in range(1, PAIRS):
                whole(nc.scalar.copy, pair, j, 0).then_inc(last_wholes, 1)
            act.wait_ge(odd_rows, 2 * pair + 1)
            for j in range(1, PAIRS):
                first_half(nc.scalar.copy, pair, j, 1)
            stage_GT(NB - LAG + 1)
            act.wait_ge(last_wholes, PAIRS - 1)
            for j in range(2, PAIRS):
                last = first_half(nc.scalar.copy, pair, j, 0)
            last.then_inc(odd_rows, 1)
            for u in range(NB, 2 * NB):
                stage_GT(u)

        @block.vector
        def _(dve):
            done = [0]

            def table_step(ins):
                done[0] += 1
                ins.then_inc(tables, 1)
                dve.wait_ge(tables, done[0])

            dve.wait_ge(A_landed, DMA)
            for version in range(2):
                turn_A(nc.vector.tensor_copy, 0, version)

            dve.wait_ge(own_steps, 3)
            dve.wait_ge(AG_done, 1)
            parts = ps_B[0][:, 0:P].rearrange("p (n m) -> p m n", n=QUADS)
            table_step(nc.vector.tensor_reduce(AG[:], parts[:, 0:E, :], AX_X, ALU.add))
            table_step(nc.vector.tensor_tensor(AG_own[:], AG[:].unsqueeze(1).to_broadcast([P, NA, E]),
                                              own[:].unsqueeze(2).to_broadcast([P, NA, E]), ALU.mult))
            assert done[0] == AG_STEPS
            dve.wait_ge(consts_made, 4)
            dve.wait_ge(ids_landed, DMA)
            table_step(nc.vector.tensor_scalar(odd_i[:], ids_sb[:], 1, None, ALU.bitwise_and))
            table_step(nc.vector.tensor_copy(odd_f[:], odd_i[:]))
            table_step(nc.vector.tensor_tensor(slot_expert[:], odd_f[:].unsqueeze(2).to_broadcast([P, NB, E]),
                                              other[:].unsqueeze(1).to_broadcast([P, NB, E]), ALU.mult))
            table_step(nc.vector.tensor_tensor(slot_expert[:], slot_expert[:],
                                              count_up[:, 0:E].unsqueeze(1).to_broadcast([P, NB, E]), ALU.add))

            def copy_xT(b, j):
                dve.wait_ge(xT_done, (b * J + j) * 2 + 2)
                nc.vector.tensor_copy(xT[:, CG:, j * P:(j + 1) * P],
                                      ps_X[1][:].rearrange("p (c t) -> p c t", c=CG)).then_inc(xT_copied[1], 1)

            def route(b):
                q = b % 2
                n = [0]

                def step(ins):
                    n[0] += 1
                    ins.then_inc(routed, 1)

                def steps_done():
                    dve.wait_ge(routed, b * ROUTE_OPS + n[0])

                dve.wait_ge(Bx_done, b + 1)
                parts = ps_B[q][:, BX_AT:].rearrange("p (j n m) -> p j m n", j=J, n=QUADS)
                step(nc.vector.tensor_reduce(Bx[q][:], parts[:, :, 0:RG, :], AX_X, ALU.add))
                steps_done()
                step(nc.vector.memset(total[:], 1.0))
                for j in range(J):
                    step(nc.vector.max(top[:, j, :], Bx[q][:, j, R:RG]))
                steps_done()
                step(nc.vector.tensor_tensor(gap[:], top[:, :, 1], top[:, :, 0], ALU.subtract))
                for j in range(J):
                    step(nc.vector.max_index(top_no[:, j, :], top[:, j, :], Bx[q][:, j, R:RG]))
                steps_done()
                step(nc.vector.tensor_copy(top_nof[:], top_no[:, :, 0:TOP]))
                steps_done()
                hot_jk = hot[:].rearrange("p j k e -> p (j k) e")
                step(nc.vector.tensor_tensor(hot_jk,
                                             slot_expert[:, b, :].unsqueeze(1).to_broadcast([P, J * TOP, E]),
                                             top_nof[:].rearrange("p j k -> p (j k)").unsqueeze(2)
                                             .to_broadcast([P, J * TOP, E]), ALU.is_equal))
                dve.wait_ge(exp_done, b + 1)
                step(nc.vector.tensor_tensor(total[:], total[:], exp_gap[:], ALU.add))
                steps_done()
                step(nc.vector.reciprocal(prob[:, :, 0], total[:]))
                steps_done()
                step(nc.vector.tensor_tensor(prob[:, :, 1], prob[:, :, 0], exp_gap[:], ALU.mult))
                steps_done()
                step(nc.vector.tensor_tensor(hot_jk, hot_jk, prob[:].rearrange("p j k -> p (j k)").unsqueeze(2)
                                             .to_broadcast([P, J * TOP, E]), ALU.mult))
                steps_done()
                step(nc.vector.tensor_tensor(w_e[:], hot[:, :, 0, :], hot[:, :, 1, :], ALU.add))
                steps_done()
                for j in range(J):
                    last = nc.vector.tensor_tensor(G[q][:, j, :, :],
                                                   Bx[q][:, j, 0:R].unsqueeze(1).to_broadcast([P, E, R]),
                                                   w_e[:, j, :].unsqueeze(2).to_broadcast([P, E, R]), ALU.mult)
                step(last)
                assert n[0] == ROUTE_OPS

            def even_adapters(pair, part):
                if part is whole:
                    dve.wait_ge(W_used, 4 * pair + 4)
                else:
                    dve.wait_ge(even_rows, 2 * pair + 1)
                    dve.wait_ge(odd_rows, 2 * pair + 1)
                for j in range(PAIRS):
                    last = part(nc.vector.tensor_copy, pair, j, 0)
                last.then_inc(even_rows, 1)

            def even_adapters_after(step):
                if step >= 1:
                    even_adapters((step - 1) // 2, whole if step % 2 else first_half)

            def add(u, q, blk):
                b = u - blk * NB
                for j in range(J):
                    dve.wait_ge(F_done, u * J + (j + 1))
                    v = x_keep[:, bass.ds(b, 1), j, blk * N:(blk + 1) * N].rearrange("p b n -> p (b n)")
                    nc.vector.tensor_tensor(v, v, ps_F[q][j][:], ALU.add).then_inc(F_added, 1)

            for b in range(NB):
                copy_xT(b, 0)
                if b:
                    route(b - 1)
                even_adapters_after(b)
                copy_xT(b, 1)
            even_adapters_after(E)
            route(NB - 1)
            dve.wait_ge(x_kept, NB)
            for step in range(E + 1, STEPS - 1):
                even_adapters_after(step)
                if step - E >= LAG:
                    add(step - E - LAG, step % 2, 0)
            last_pair = STEPS // 2 - 1
            dve.wait_ge(W_used, 2 * STEPS)
            whole(nc.vector.tensor_copy, last_pair, 0, 0).then_inc(even_rows, 1)
            dve.wait_ge(odd_rows, 2 * last_pair + 1)
            first_half(nc.vector.tensor_copy, last_pair, 0, 1)
            dve.wait_ge(last_wholes, 1)
            dve.wait_ge(even_rows, 2 * last_pair + 1)
            for j in range(2):
                last = first_half(nc.vector.tensor_copy, last_pair, j, 0)
            last.then_inc(even_rows, 1)
            add(NB - LAG - 1, (NB - LAG - 1) % 2, 0)
            for u in range(NB - LAG, NB):
                add(u, u % 2, 0)
            with dve.Fori(PAIRS, 2 * PAIRS) as trip:
                for q in range(2):
                    add(trip * 2 + q, q, 1)

        @block.tensor
        def _(pe):
            def experts_product(trip, q, half, waits, begin=0, end=HALF):
                n = 2 * q + half
                out_bank = ps_P[:, bass.ds((trip & 1) * 2 + q, 1), :].rearrange("p b n -> p (b n)")
                if waits and (q, half) == (0, 0):
                    pe.wait_ge(odd_rows, trip * 2 - 2)
                    pe.wait_ge(even_rows, trip * 2 - 2)
                if end == HALF:
                    pe.wait_ge(W_landed[n], trip * DMA + DMA)
                for k in range(begin, end):
                    kk = half * HALF + k
                    last = nc.tensor.matmul(out_bank, A_T[q][:, kk, :], W_sb[n][:, k, :],
                                            start=(kk == 0), stop=(kk == K - 1))
                if end == HALF:
                    last.then_inc(W_used, 1)

            def x_transposes(trip, q, j):
                b = trip * 2 + q
                if j == 0:
                    pe.wait_ge(x_landed[q], trip * DMA + DMA)
                for g in range(2):
                    if not (isinstance(b, int) and b == 0 and j == 0):
                        pe.wait_ge(xT_copied[g], b * J + j)
                    for c in range(CG):
                        cc = g * CG + c
                        last = nc.tensor.transpose(ps_X[g][:, c * P:(c + 1) * P],
                                                   x_in[q][:, j, cc * P:(cc + 1) * P], ident[:])
                    last.then_inc(xT_done, 1)

            def BxT_product(trip, q):
                b = trip * 2 + q
                pe.wait_ge(BG_staged, b + 1)
                for g in range(2):
                    pe.wait_ge(xT_copied[g], b * J + J)
                if not (isinstance(trip, int) and trip == 0):
                    pe.wait_ge(GT_copied, b - 1)
                for c in range(C):
                    n = c % QUADS
                    part = nc.tensor.matmul(ps_B[q][n * Q:(n + 1) * Q, 0:J * P], BG_now[q][:, c, :], xT[:, c, :],
                                            start=(c < QUADS), stop=(c >= C - QUADS), tile_position=(0, n * Q))
                    if c >= C - QUADS:
                        part.then_inc(BxT_done, 1)

            def Bx_transposes(b, q):
                pe.wait_ge(BxT_copied, b + 1)
                for j in range(J):
                    last = nc.tensor.transpose(ps_B[q][:, BX_AT + j * P:BX_AT + (j + 1) * P],
                                               BxT[:, j * P:(j + 1) * P], ident[:])
                last.then_inc(Bx_done, 1)

            def g_transposes(b, q):
                pe.wait_ge(routed, b * ROUTE_OPS + ROUTE_OPS)
                for j in range(J):
                    last = nc.tensor.transpose(ps_B[q][:, j * P:(j + 1) * P],
                                               G[q][:, j, :, :].rearrange("p e r -> p (e r)"), ident[:])
                last.then_inc(GT_done, 1)

            def x_step(trip, q):
                experts = (trip, 1) if q == 0 else (trip + 1, 0)
                x_transposes(trip, q, 0)
                Bx_transposes(trip * 2 + (q - 1), 1 - q)
                experts_product(*experts, 0, not (isinstance(trip, int) and trip == 0))
                x_transposes(trip, q, 1)
                experts_product(*experts, 1, False)
                g_transposes(trip * 2 + (q - 1), 1 - q)
                BxT_product(trip, q)

            def first_x_step():
                experts_product(0, 1, 0, False)
                x_transposes(0, 0, 0)
                pe.wait_ge(W_landed[3], DMA)
                experts_product(0, 1, 1, False, 0, BEGIN)
                x_transposes(0, 0, 1)
                experts_product(0, 1, 1, False, BEGIN, HALF)
                BxT_product(0, 0)

            def final(trip, q, blk, waits):
                u = trip * 2 + q
                a = pe.value_load(ids_sb[0:1, bass.ds(u - blk * NB, 1)], min_val=0, max_val=NA - 1)
                pe.wait_ge(GT_staged, u + 1)
                for j in range(J):
                    if waits:
                        pe.wait_ge(F_added, u * J + (j + 1 - 2 * J))
                    nc.tensor.matmul(ps_F[q][j][:], GT_now[q][:, j, :],
                                     M_sb[:, bass.ds(a + blk * NA, 1), :].rearrange("p b n -> p (b n)"),
                                     start=True, stop=True).then_inc(F_done, 1)

            def warm(products):
                for _ in range(products):
                    nc.tensor.matmul(ps_X[0][:, 0:P], ident[:], ident[:], start=True, stop=True)

            pe.wait_ge(consts_made, 1)
            warm(WARM_UP)
            pe.wait_ge(gate_widened, 1)
            for k in range(K):
                if k % HALF == 0:
                    pe.wait_ge(A_turned[k // HALF], 1)
                n = k % QUADS
                part = nc.tensor.matmul(ps_B[1][n * Q:(n + 1) * Q, 0:P], gate_wide[:, k, :], A_T[0][:, k, :],
                                        start=(k < QUADS), stop=(k >= K - QUADS), tile_position=(0, n * Q))
                if k >= K - QUADS:
                    part.then_inc(AG_T_done, 1)
            warm(KEEP_WARM)
            pe.wait_ge(AG_T_copied, 1)
            nc.tensor.transpose(ps_B[0][:, 0:P], AG_T[:], ident[:]).then_inc(AG_done, 1)
            pe.wait_ge(W_begun, DMA)
            experts_product(0, 0, 0, False, 0, BEGIN)
            experts_product(0, 0, 0, False, BEGIN, HALF)
            experts_product(0, 0, 1, False)
            pe.wait_ge(B_landed, DMA)
            pe.wait_ge(tables, AG_STEPS)
            for n, ps in enumerate(BG_banks):
                for c in range(2):
                    chunk = B_sb[:, (2 * n + c) * P:(2 * n + c + 1) * P]
                    at = c * (P + NA * E)
                    nc.tensor.transpose(ps[:, at:at + P], chunk, ident[:])
                    last = nc.tensor.matmul(ps[:, at + P:at + P + NA * E], chunk,
                                            AG_own[:].rearrange("p a e -> p (a e)"), start=True, stop=True)
                last.then_inc(BG_done, 1)

            for half in range(2):
                pe.wait_ge(A_turned[half], 3)
            first_x_step()
            x_step(0, 1)
            with pe.Fori(1, PAIRS) as trip:
                for q in range(2):
                    x_step(trip, q)

            experts_product(PAIRS, 1, 0, True)
            Bx_transposes(NB - 1, 1)
            experts_product(PAIRS, 1, 1, True)

            def block1_trip(trip, final_waits):
                for q in range(2):
                    experts_product(trip, q, 0, True)
                    if not final_waits and q == 0:
                        g_transposes(NB - 1, 1)
                    experts_product(trip, q, 1, True)
                    final(trip - (PAIRS + LAG // 2), q, 0, final_waits)

            pe.wait_ge(ids_landed, DMA)
            block1_trip(PAIRS + 1, False)
            with pe.Fori(PAIRS + 2, 2 * PAIRS) as trip:
                block1_trip(trip, True)
            for q in range(2):
                final(PAIRS - 1, q, 0, True)
            pe.wait_ge(odd_rows, STEPS)
            pe.wait_ge(even_rows, STEPS)
            for q in range(2):
                final(PAIRS, q, 1, True)
            with pe.Fori(PAIRS + 1, 2 * PAIRS) as trip:
                for q in range(2):
                    final(trip, q, 1, True)


def kernel(x, itok_B_3_7, L0_cond_A, L0_cond_B, L0_ffn_gate_w, L0_ffn_expert_w):
    import numpy as np
    import concourse.bacc as bacc
    from concourse.bass_utils import run_bass_kernel_spmd

    nc = bacc.Bacc("TRN2", target_bir_lowering=False, num_devices=1)
    given = {"x": x, "ids": itok_B_3_7, "A": L0_cond_A, "B": L0_cond_B, "gate_w": L0_ffn_gate_w,
             "W": L0_ffn_expert_w}
    arrays, args = {}, []
    for name, a in given.items():
        a = np.ascontiguousarray(a)
        arrays[f"{name}_dram"] = a
        args.append(nc.dram_tensor(f"{name}_dram", a.shape, mybir.dt.from_np(a.dtype), kind="ExternalInput").ap())
    result = nc.dram_tensor("out_dram", arrays["x_dram"].shape, F32, kind="ExternalOutput").ap()
    adaln_ffn(nc, *args, result)
    r = run_bass_kernel_spmd(nc, [arrays], core_ids=[0])
    return r.results[0]["out_dram"]
```
